# Optimizing a Trainium2 kernel written in Bass

```python
import numpy as np
import jax
import jax.numpy as jnp

def _softmax(x, axis=-1):
    return jax.nn.softmax(x, axis=axis)

def _gelu(x):
    return jax.nn.gelu(x, approximate=True)

def _silu(x):
    return jax.nn.silu(x)

def _sigmoid(x):
    return jax.nn.sigmoid(x)

def _layernorm(x, axis=-1, eps=1e-05):
    m = jnp.mean(x, axis=axis, keepdims=True)
    v = jnp.var(x, axis=axis, keepdims=True)
    return (x - m) / jnp.sqrt(v + eps)

def _scatter_add(tgt, idx, src, axis=0):
    return tgt.at[idx].add(src)

def _segment_sum(src, seg, n):
    return jax.ops.segment_sum(src, seg, n)
kernel_name = 'mk_early_fusion_embed_d1_tok_img768_r4_48d7e0'

def setup_inputs(seed: int=0):
    np.random.seed(seed)
    _w = jnp.asarray

    def _rec_inputs():
        import jax
        import jax.numpy as jnp
        _rk = jax.random.key(seed)
        x = -0.000222058 + 0.999998 * jax.random.normal(jax.random.fold_in(_rk, 1), (64, 3, 224, 224), jnp.float32)
        x_txt = jax.random.randint(jax.random.fold_in(_rk, 51), (64, 128), 0, 12564, jnp.int32)
        return (x, x_txt)
    x, x_txt = _rec_inputs()

    def _L0_tok_setup():
        import jax, jax.numpy as jnp
        import numpy as np
        from jax import lax
        HIDDEN = 192
        C_IN = 3
        PATCH = 16
        SIDE = 32
        NUM_PATCHES = SIDE * SIDE

        def _position_ids(nb_h, nb_w):
            boundaries = np.arange(1.0 / SIDE, 1.0, 1.0 / SIDE, dtype=np.float32)
            frac_h = np.arange(0.0, 1.0 - 1e-06, 1.0 / nb_h, dtype=np.float32)
            frac_w = np.arange(0.0, 1.0 - 1e-06, 1.0 / nb_w, dtype=np.float32)
            bh = np.searchsorted(boundaries, frac_h, side='right')
            bw = np.searchsorted(boundaries, frac_w, side='right')
            return jnp.asarray((bh[:, None] * SIDE + bw).reshape(-1), dtype=jnp.int32)
        key = jax.random.key(seed)
        k1, k2, k3 = jax.random.split(key, 3)
        pixel_values = jax.random.normal(k1, (32, C_IN, 128, 128), dtype=jnp.float32)
        conv_w = jax.random.normal(k2, (HIDDEN, C_IN, PATCH, PATCH), dtype=jnp.float32) * 0.02
        conv_b = jnp.zeros((HIDDEN,), dtype=jnp.float32)
        pos_table = jax.random.normal(k3, (NUM_PATCHES, HIDDEN), dtype=jnp.float32) * 0.02
        return {'pixel_values': pixel_values, 'conv_w': conv_w, 'conv_b': conv_b, 'pos_table': pos_table}
    _L0_tok_all = _L0_tok_setup()
    _L0_tok_in = {k: v for k, v in _L0_tok_all.items() if k in ('conv_w', 'conv_b', 'pos_table')}
    del _L0_tok_all

    def _L0_txt_setup():
        import jax, jax.numpy as jnp
        import numpy as np
        B, T, V, C = (8, 512, 50257, 192)

        def _rosa(x):
            Bx, Tx = x.shape
            eq = (x[:, :, None] == x[:, None, :]).astype(jnp.int32)

            def step(prev, eq_row):
                cur = (jnp.pad(prev[:, :-1], ((0, 0), (1, 0))) + 1) * eq_row
                return (cur, cur)
            init = jnp.zeros((Bx, Tx), jnp.int32)
            _, rows = jax.lax.scan(step, init, jnp.swapaxes(eq, 0, 1)[1:])
            L = jnp.swapaxes(jnp.concatenate([init[None], rows], axis=0), 0, 1)
            mask = jnp.tril(jnp.ones((Tx, Tx), dtype=bool), -1)
            j = jnp.arange(Tx, dtype=jnp.float32)
            TIE = 1e-05
            scored = jnp.where(mask[None], L.astype(jnp.float32) + j[None, None, :] * TIE, -1.0)
            best_j = jnp.argmax(scored, axis=2)
            pred_idx = jnp.minimum(best_j + 1, Tx - 1)
            preds = jnp.take_along_axis(x, pred_idx, axis=1)
            no_match = jnp.max(jnp.where(mask[None], L, 0), axis=2) == 0
            return jnp.where(no_match, -1, preds)
        key = jax.random.key(seed)
        k1, k2 = jax.random.split(key)
        idx = jax.random.randint(k1, (B, T), 0, V)
        emb = jax.random.normal(k2, (V, C), dtype=jnp.float32)
        return {'idx': idx, 'emb': emb}
    _L0_txt_all = _L0_txt_setup()
    _L0_txt_in = {k: v for k, v in _L0_txt_all.items() if k in ('emb',)}
    del _L0_txt_all

    def _L0_attn_setup():
        import jax, jax.numpy as jnp
        import numpy as np

        def _selective_scan(dt, Bm, Cm, xp, A):
            Bsz, L, d_inner = xp.shape
            N = A.shape[1]

            def step(h, inp):
                dt_t, B_t, C_t, x_t = inp
                dA = jnp.exp(dt_t[..., None] * A)
                dBx = (dt_t * x_t)[..., None] * B_t[:, None, :]
                h = dA * h + dBx
                y = jnp.einsum('bdn,bn->bd', h, C_t)
                return (h, y)
            h0 = jnp.zeros((Bsz, d_inner, N), dtype=xp.dtype)
            inputs = (jnp.moveaxis(dt, 1, 0), jnp.moveaxis(Bm, 1, 0), jnp.moveaxis(Cm, 1, 0), jnp.moveaxis(xp, 1, 0))
            _, ys = jax.lax.scan(step, h0, inputs)
            return jnp.moveaxis(ys, 0, 1)
        key = jax.random.key(seed)
        ks = jax.random.split(key, 9)
        B, L, D = (2, 512, 192)
        d_inner, N, R = (384, 16, 48)
        s = 0.02
        x = jax.random.normal(ks[0], (B, L, D), dtype=jnp.float32)
        W_in = jax.random.normal(ks[1], (D, 2 * d_inner), dtype=jnp.float32) * s
        W_x = jax.random.normal(ks[2], (d_inner, R + 2 * N), dtype=jnp.float32) * s
        W_dt = jax.random.normal(ks[3], (R, d_inner), dtype=jnp.float32) * s
        b_dt = jax.random.normal(ks[4], (d_inner,), dtype=jnp.float32) * s
        A_log = jnp.log(jnp.broadcast_to(jnp.arange(1, N + 1, dtype=jnp.float32), (d_inner, N)))
        D_skip = jnp.ones((d_inner,), dtype=jnp.float32)
        W_out = jax.random.normal(ks[5], (d_inner, D), dtype=jnp.float32) * s
        gamma = jnp.ones((D,), dtype=jnp.float32)
        beta = jnp.zeros((D,), dtype=jnp.float32)
        return {'x': x, 'W_in': W_in, 'W_x': W_x, 'W_dt': W_dt, 'b_dt': b_dt, 'A_log': A_log, 'D_skip': D_skip, 'W_out': W_out, 'gamma': gamma, 'beta': beta}
    _L0_attn_all = _L0_attn_setup()
    _L0_attn_in = {k: v for k, v in _L0_attn_all.items() if k in ('W_in', 'W_x', 'W_dt', 'b_dt', 'A_log', 'D_skip', 'W_out', 'gamma', 'beta')}
    del _L0_attn_all

    def _L0_ffn_setup():
        import math
        import jax, jax.numpy as jnp
        import numpy as np
        EMBED_CHOICES = [96, 144, 192]
        RATIO_CHOICES = [2, 3, 4]
        E_MAX = 192
        H_MAX = 768

        def new_gelu(x):
            c = math.sqrt(2.0 / math.pi)
            return 0.5 * x * (1.0 + jnp.tanh(c * (x + 0.044715 * x * x * x)))

        def _mixed_coeffs(alpha_e, alpha_r):
            h_idx = jnp.arange(H_MAX)
            d_idx = jnp.arange(E_MAX)
            C0 = jnp.zeros((H_MAX, E_MAX), jnp.float32)
            c0b = jnp.zeros((H_MAX,), jnp.float32)
            C1 = jnp.zeros((E_MAX, H_MAX), jnp.float32)
            c1b = jnp.zeros((E_MAX,), jnp.float32)
            for i, e in enumerate(EMBED_CHOICES):
                m_in = (d_idx < e).astype(jnp.float32)
                for j, r in enumerate(RATIO_CHOICES):
                    a = alpha_e[i] * alpha_r[j]
                    m_out = (h_idx < r * e).astype(jnp.float32)
                    C0 = C0 + a * (m_out[:, None] * m_in[None, :])
                    c0b = c0b + a * m_out
                    C1 = C1 + a * (m_in[:, None] * m_out[None, :])
                    c1b = c1b + a * m_in
            return (C0, c0b, C1, c1b)
        key = jax.random.key(seed)
        ks = jax.random.split(key, 6)
        x = jax.random.normal(ks[0], (8, 512, E_MAX), jnp.float32)
        w_fc = jax.random.normal(ks[1], (H_MAX, E_MAX), jnp.float32) * 0.02
        b_fc = jnp.zeros((H_MAX,), jnp.float32)
        w_proj = jax.random.normal(ks[2], (E_MAX, H_MAX), jnp.float32) * 0.02
        b_proj = jnp.zeros((E_MAX,), jnp.float32)
        alpha_e = jax.nn.softmax(jax.random.normal(ks[3], (3,), jnp.float32))
        alpha_r = jax.nn.softmax(jax.random.normal(ks[4], (3,), jnp.float32))
        return {'x': x, 'w_fc': w_fc, 'b_fc': b_fc, 'w_proj': w_proj, 'b_proj': b_proj, 'alpha_e': alpha_e, 'alpha_r': alpha_r}
    _L0_ffn_all = _L0_ffn_setup()
    _L0_ffn_in = {k: v for k, v in _L0_ffn_all.items() if k in ('w_fc', 'b_fc', 'w_proj', 'b_proj', 'alpha_e', 'alpha_r')}
    del _L0_ffn_all
    return {'x': x, 'x_txt': x_txt, 'L0_tok_conv_w': _L0_tok_in['conv_w'], 'L0_tok_conv_b': _L0_tok_in['conv_b'], 'L0_tok_pos_table': _L0_tok_in['pos_table'], 'L0_txt_emb': _L0_txt_in['emb'], 'L0_attn_W_in': _L0_attn_in['W_in'], 'L0_attn_W_x': _L0_attn_in['W_x'], 'L0_attn_W_dt': _L0_attn_in['W_dt'], 'L0_attn_b_dt': _L0_attn_in['b_dt'], 'L0_attn_A_log': _L0_attn_in['A_log'], 'L0_attn_D_skip': _L0_attn_in['D_skip'], 'L0_attn_W_out': _L0_attn_in['W_out'], 'L0_attn_gamma': _L0_attn_in['gamma'], 'L0_attn_beta': _L0_attn_in['beta'], 'L0_ffn_w_fc': _L0_ffn_in['w_fc'], 'L0_ffn_b_fc': _L0_ffn_in['b_fc'], 'L0_ffn_w_proj': _L0_ffn_in['w_proj'], 'L0_ffn_b_proj': _L0_ffn_in['b_proj'], 'L0_ffn_alpha_e': _L0_ffn_in['alpha_e'], 'L0_ffn_alpha_r': _L0_ffn_in['alpha_r']}

def reference(x, x_txt, L0_tok_conv_w, L0_tok_conv_b, L0_tok_pos_table, L0_txt_emb, L0_attn_W_in, L0_attn_W_x, L0_attn_W_dt, L0_attn_b_dt, L0_attn_A_log, L0_attn_D_skip, L0_attn_W_out, L0_attn_gamma, L0_attn_beta, L0_ffn_w_fc, L0_ffn_b_fc, L0_ffn_w_proj, L0_ffn_b_proj, L0_ffn_alpha_e, L0_ffn_alpha_r):
    import jax
    import jax.numpy as jnp

    def _L0_tok_ref(pixel_values, conv_w, conv_b, pos_table):
        import jax, jax.numpy as jnp
        import numpy as np
        from jax import lax
        HIDDEN = 192
        C_IN = 3
        PATCH = 16
        SIDE = 32
        NUM_PATCHES = SIDE * SIDE

        def _position_ids(nb_h, nb_w):
            boundaries = np.arange(1.0 / SIDE, 1.0, 1.0 / SIDE, dtype=np.float32)
            frac_h = np.arange(0.0, 1.0 - 1e-06, 1.0 / nb_h, dtype=np.float32)
            frac_w = np.arange(0.0, 1.0 - 1e-06, 1.0 / nb_w, dtype=np.float32)
            bh = np.searchsorted(boundaries, frac_h, side='right')
            bw = np.searchsorted(boundaries, frac_w, side='right')
            return jnp.asarray((bh[:, None] * SIDE + bw).reshape(-1), dtype=jnp.int32)
        B, _, H, W = pixel_values.shape
        nb_h, nb_w = (H // PATCH, W // PATCH)
        patches = lax.conv_general_dilated(pixel_values, conv_w, window_strides=(PATCH, PATCH), padding='VALID', dimension_numbers=('NCHW', 'OIHW', 'NCHW'))
        patches = patches + conv_b[None, :, None, None]
        embeddings = patches.reshape(B, HIDDEN, nb_h * nb_w).transpose(0, 2, 1)
        pos_ids = _position_ids(nb_h, nb_w)
        pos_emb = pos_table[pos_ids]
        return embeddings + pos_emb[None, :, :]

    def _L0_txt_ref(idx, emb):
        import jax, jax.numpy as jnp
        import numpy as np
        B, T, V, C = (8, 512, 50257, 192)

        def _rosa(x):
            Bx, Tx = x.shape
            eq = (x[:, :, None] == x[:, None, :]).astype(jnp.int32)

            def step(prev, eq_row):
                cur = (jnp.pad(prev[:, :-1], ((0, 0), (1, 0))) + 1) * eq_row
                return (cur, cur)
            init = jnp.zeros((Bx, Tx), jnp.int32)
            _, rows = jax.lax.scan(step, init, jnp.swapaxes(eq, 0, 1)[1:])
            L = jnp.swapaxes(jnp.concatenate([init[None], rows], axis=0), 0, 1)
            mask = jnp.tril(jnp.ones((Tx, Tx), dtype=bool), -1)
            j = jnp.arange(Tx, dtype=jnp.float32)
            TIE = 1e-05
            scored = jnp.where(mask[None], L.astype(jnp.float32) + j[None, None, :] * TIE, -1.0)
            best_j = jnp.argmax(scored, axis=2)
            pred_idx = jnp.minimum(best_j + 1, Tx - 1)
            preds = jnp.take_along_axis(x, pred_idx, axis=1)
            no_match = jnp.max(jnp.where(mask[None], L, 0), axis=2) == 0
            return jnp.where(no_match, -1, preds)
        p = _rosa(idx)
        out = emb[jnp.clip(p, 0)]
        return jnp.where((p == -1)[..., None], 0.0, out)

    def _L0_attn_ref(x, W_in, W_x, W_dt, b_dt, A_log, D_skip, W_out, gamma, beta):
        import jax, jax.numpy as jnp
        import numpy as np

        def _selective_scan(dt, Bm, Cm, xp, A):
            Bsz, L, d_inner = xp.shape
            N = A.shape[1]

            def step(h, inp):
                dt_t, B_t, C_t, x_t = inp
                dA = jnp.exp(dt_t[..., None] * A)
                dBx = (dt_t * x_t)[..., None] * B_t[:, None, :]
                h = dA * h + dBx
                y = jnp.einsum('bdn,bn->bd', h, C_t)
                return (h, y)
            h0 = jnp.zeros((Bsz, d_inner, N), dtype=xp.dtype)
            inputs = (jnp.moveaxis(dt, 1, 0), jnp.moveaxis(Bm, 1, 0), jnp.moveaxis(Cm, 1, 0), jnp.moveaxis(xp, 1, 0))
            _, ys = jax.lax.scan(step, h0, inputs)
            return jnp.moveaxis(ys, 0, 1)
        R = W_dt.shape[0]
        N = A_log.shape[1]
        d_inner = A_log.shape[0]
        xz = jnp.einsum('bld,de->ble', x, W_in)
        xp, z = (xz[..., :d_inner], xz[..., d_inner:])
        xp = jax.nn.silu(xp)
        x_dbl = jnp.einsum('bld,dr->blr', xp, W_x)
        dt = jax.nn.softplus(jnp.einsum('blr,rd->bld', x_dbl[..., :R], W_dt) + b_dt)
        Bm = x_dbl[..., R:R + N]
        Cm = x_dbl[..., R + N:]
        A = -jnp.exp(A_log)
        ys = _selective_scan(dt, Bm, Cm, xp, A)
        y = (ys + D_skip * xp) * jax.nn.silu(z)
        mamba_out = jnp.einsum('bld,de->ble', y, W_out)
        h = x + mamba_out
        mu = jnp.mean(h, axis=-1, keepdims=True)
        var = jnp.mean(jnp.square(h - mu), axis=-1, keepdims=True)
        return (h - mu) * jax.lax.rsqrt(var + 1e-05) * gamma + beta

    def _L0_ffn_ref(x, w_fc, b_fc, w_proj, b_proj, alpha_e, alpha_r):
        import math
        import jax, jax.numpy as jnp
        import numpy as np
        EMBED_CHOICES = [96, 144, 192]
        RATIO_CHOICES = [2, 3, 4]
        E_MAX = 192
        H_MAX = 768

        def new_gelu(x):
            c = math.sqrt(2.0 / math.pi)
            return 0.5 * x * (1.0 + jnp.tanh(c * (x + 0.044715 * x * x * x)))

        def _mixed_coeffs(alpha_e, alpha_r):
            h_idx = jnp.arange(H_MAX)
            d_idx = jnp.arange(E_MAX)
            C0 = jnp.zeros((H_MAX, E_MAX), jnp.float32)
            c0b = jnp.zeros((H_MAX,), jnp.float32)
            C1 = jnp.zeros((E_MAX, H_MAX), jnp.float32)
            c1b = jnp.zeros((E_MAX,), jnp.float32)
            for i, e in enumerate(EMBED_CHOICES):
                m_in = (d_idx < e).astype(jnp.float32)
                for j, r in enumerate(RATIO_CHOICES):
                    a = alpha_e[i] * alpha_r[j]
                    m_out = (h_idx < r * e).astype(jnp.float32)
                    C0 = C0 + a * (m_out[:, None] * m_in[None, :])
                    c0b = c0b + a * m_out
                    C1 = C1 + a * (m_in[:, None] * m_out[None, :])
                    c1b = c1b + a * m_in
            return (C0, c0b, C1, c1b)
        C0, c0b, C1, c1b = _mixed_coeffs(alpha_e, alpha_r)
        W0 = w_fc * C0
        b0 = b_fc * c0b
        h = jnp.einsum('bte,he->bth', x, W0) + b0
        h = new_gelu(h)
        W1 = w_proj * C1
        b1 = b_proj * c1b
        out = jnp.einsum('bth,eh->bte', h, W1) + b1
        return out
    h = _L0_tok_ref(x, L0_tok_conv_w, L0_tok_conv_b, L0_tok_pos_table)
    h = jnp.concatenate([h, _L0_txt_ref(x_txt, L0_txt_emb)], axis=1)
    h = h + _L0_attn_ref(_layernorm(h, axis=-1), L0_attn_W_in, L0_attn_W_x, L0_attn_W_dt, L0_attn_b_dt, L0_attn_A_log, L0_attn_D_skip, L0_attn_W_out, L0_attn_gamma, L0_attn_beta)
    h = h + _L0_ffn_ref(_layernorm(h, axis=-1), L0_ffn_w_fc, L0_ffn_b_fc, L0_ffn_w_proj, L0_ffn_b_proj, L0_ffn_alpha_e, L0_ffn_alpha_r)
    return h

_drawn_inputs = setup_inputs


def setup_inputs(seed=0):
    import zlib

    import numpy as np

    out = dict(_drawn_inputs(seed))
    spreads = {'L0_tok_conv_b': (0.0, 0.1),
     'L0_attn_D_skip': (1.0, 0.6),
     'L0_attn_gamma': (1.0, 0.2),
     'L0_attn_beta': (0.0, 0.1),
     'L0_ffn_b_fc': (0.0, 0.531),
     'L0_ffn_b_proj': (0.0, 0.1)}
    factors = {'L0_attn_W_in': 8.0,
     'L0_attn_W_x': 8.0,
     'L0_attn_W_dt': 8.0,
     'L0_attn_b_dt': 45.085,
     'L0_attn_A_log': 8.0,
     'L0_attn_W_out': 8.0,
     'L0_ffn_alpha_r': 6.206}
    for name, (base, spread) in spreads.items():
        noise = np.random.default_rng([zlib.crc32(name.encode()), seed]).standard_normal(out[name].shape)
        drawn = base * np.exp(spread * noise) if base else spread * noise
        out[name] = jnp.asarray(drawn.astype(out[name].dtype))
    for name, factor in factors.items():
        out[name] = (out[name] * factor).astype(out[name].dtype)
    return out
```

```python
from contextlib import ExitStack

import concourse.bass as bass
from concourse import mybir

F32 = mybir.dt.float32
BF16 = mybir.dt.bfloat16
I32 = mybir.dt.int32
ALU = mybir.AluOpType
ACT = mybir.ActivationFunctionType
AX = mybir.AxisListType

P = 128
BANK = 512
PATCH = 16
EPS = 1e-5
EMBED_CHOICES = (96, 144, 192)
RATIO_CHOICES = (2, 3, 4)
NO_ROW = 1 << 20

AHEAD = {"P": 2, "T": 2, "M": 6, "X": 2, "D": 3}
BEHIND = {"O": 2, "U": 2, "F": 6, "G": 2}
ORDER = (["P0", "P1", "O0", "O1", "T0", "T1"] + [f"M{m}" for m in range(6)] + ["U0", "U1"]
         + [f"F{m}" for m in range(6)] + ["X0", "X1", "D0", "D1", "D2", "G0", "G1"])
WORK = 3
PAIRS = 16
UNITS = 12
RING = 4


class Batch:

    def __init__(self, o, it=None):
        self.o, self.it, self.par = o, it, o % 2

    def plus(self, k):
        return Batch(self.o + k, self.it)

    def index(self):
        return self.o if self.it is None else self.it * 2 + self.o

    def count(self, per, n):
        c = per * self.o + n
        if self.it is None:
            return max(c, 0)
        assert c >= 0
        return self.it * (2 * per) + c

    def pair_count(self, per):
        c = per * (self.o // 2)
        if self.it is None:
            return max(c, 0)
        assert c >= 0
        return self.it * per + c


class Step:

    def __init__(self, batch, first, ahead=True, scan=True, behind=True):
        self.batch, self.ahead, self.scan, self.behind = batch, ahead, scan, behind
        kinds = (AHEAD if ahead else {}) | (BEHIND if behind else {})
        self.items = {x: first + i for i, x in enumerate(x for x in ORDER if x[0] in kinds)}
        self.end = first + len(self.items)

    def work(self, item, it="own"):
        n = self.items[item]
        it = self.batch.it if isinstance(it, str) else it
        uses = n // WORK
        return n % WORK, uses if it is None else it * (2 * len(ORDER) // WORK) + uses


def wait(eng, sem, value):
    if not (isinstance(value, int) and value <= 0):
        eng.wait_ge(sem, value)


def build(nc, img_d, txt_d, convw_d, convb_d, pos_d, posid_d, emb_d, win_d, wx_d, wdt_d, bdt_d, alog_d, dskip_d,
          wout_d, gamma_d, beta_d, wfcT_d, bfc_d, wprojT_d, bproj_d, ae_d, ar_d, out_d):
    NB, _, KT, NPATCH = img_d.shape
    NTXT = txt_d.shape[1]
    NTOK, C = out_d.shape[1:]
    DI, NS = alog_d.shape
    R = wdt_d.shape[0]
    H = wfcT_d.shape[1]
    V = emb_d.shape[0]
    TP = NPATCH // 2
    TOK = [(0, TP), (TP, TP), (NPATCH, NTXT)]
    KD = DI // P
    KH = H // P
    CH = C // 2
    NQ = 4
    QS = NS // NQ
    IMGW = KT * NPATCH + P - TP + (NPATCH - 2 * TP)
    assert NTXT == P and KD == 3 and NQ * KD == UNITS and NQ * 4 == PAIRS and 2 * CH == C and NB % 2 == 0

    with ExitStack() as ctx:
        def sb(name, shape, dt=F32):
            return ctx.enter_context(nc.sbuf_tensor(name, shape, dt))

        def sem(name):
            return ctx.enter_context(nc.semaphore(name))

        y_ps = ctx.enter_context(nc.psum_tensor("y_ps", [P, KD, BANK], F32))
        row_ps = ctx.enter_context(nc.psum_tensor("row_ps", [P, 2, BANK], F32))
        work = [ctx.enter_context(nc.psum_tensor(f"work{i}", [P, BANK], F32)) for i in range(WORK)]

        ident = sb("ident", [P, P])
        row_sel = sb("row_sel", [96, 2 * NS, P], BF16)
        convw = sb("convw", [P, KT, C])
        pos = sb("pos", [P, 2, C])
        w_in = sb("w_in", [CH, 2, 2 * DI])
        w_dt_rows = sb("w_dt_rows", [P, KD, R])
        w_bc = sb("w_bc", [P, KD, 3, 2 * NS])
        w_dt = sb("w_dt", [R, DI])
        b_dt = sb("b_dt", [P, KD])
        d_half = sb("d_half", [P, KD])
        A = sb("A", [P, KD, NS])
        w_out = sb("w_out", [P, KD, C])
        gamma = sb("gamma", [P, C])
        beta = sb("beta", [P, C])
        w0 = sb("w0", [CH, 2, H])
        b0 = sb("b0", [P, KH])
        w1 = sb("w1", [P, KH, C])
        b1 = sb("b1", [P, C])
        row_table = sb("row_table", [P, NB], I32)
        minus_half = sb("minus_half", [P, 3])
        small = sb("small", [P, 128])
        padded = sb("padded", [P, NTXT + 64], I32)

        img = sb("img", [P, 2, IMGW])
        h = sb("h", [P, 2, 3, C])
        xn = sb("xn", [P, 2, 3, C])
        h_post = sb("h_post", [P, 3, C])
        x_post = sb("x_post", [P, 3, C])
        res = sb("res", [P, 3, C])
        xn2 = sb("xn2", [P, 3, C])
        obuf = sb("obuf", [P, 2, 3, C])
        txt_row = sb("txt_row", [P, 1], I32)
        txt_tok = sb("txt_tok", [P, 1], I32)
        txt_emb = sb("txt_emb", [P, C])
        stats = sb("stats", [P, 3, 3, 6])
        mv = sb("mv", [P, 3, 3, 2])
        veps = sb("veps", [P, 3, 3])
        rstd = sb("rstd", [P, 3, 3])
        xT = sb("xT", [CH, 2, NTOK])
        x2T = sb("x2T", [CH, 2, NTOK])
        th = sb("th", [P, 2 * KD, NTOK])
        xz = sb("xz", [P, 2, 2 * KD, NTOK])
        dt_rows = sb("dt_rows", [R, NTOK])
        bc3 = sb("bc3", [96, 2, NTOK], BF16)
        bc_rest = sb("bc_rest", [96, NTOK])
        bc_mid = sb("bc_mid", [96, NTOK], BF16)
        relu = sb("relu", [P, KD, NTOK])
        corr = sb("corr", [P, KD, NTOK])
        dt = sb("dt", [P, 2, KD, NTOK])
        u = sb("u", [P, 2, KD, NTOK])
        rings = sb("rings", [P, 2, RING, QS * NTOK])
        dA = rings[:, 0, :, :].rearrange("p r (n t) -> p r n t", n=QS)
        st = rings[:, 1, :, :].rearrange("p r (n t) -> p r n t", n=QS)
        Bq = sb("Bq", [P, 2, QS, NTOK])
        Cq = sb("Cq", [P, 2, QS, NTOK])
        yz = sb("yz", [P, KD, NTOK])
        gT = sb("gT", [P, KH, NTOK])

        filled = [sem(f"filled{i}") for i in range(WORK)]
        drained = [sem(f"drained{i}") for i in range(WORK)]
        img_in = [sem(f"img_in{i}") for i in range(2)]
        out_stored = [sem(f"out_stored{i}") for i in range(2)]
        row_ready = sem("row_ready")
        tok_in = sem("tok_in")
        emb_in = sem("emb_in")
        txt_copied = sem("txt_copied")
        posted = sem("posted")
        stat_done = [sem(f"stat_done{i}") for i in range(3)]
        mv_done = [sem(f"mv_done{i}") for i in range(3)]
        veps_done = [sem(f"veps_done{i}") for i in range(3)]
        rstd_done = [sem(f"rstd_done{i}") for i in range(3)]
        xn_done = sem("xn_done")
        th_done = sem("th_done")
        bc_hi = sem("bc_hi")
        bc_q = sem("bc_q")
        bc_lo = sem("bc_lo")
        abs_done = sem("abs_done")
        sp_act = sem("sp_act")
        sp_pool = sem("sp_pool")
        dt_done = sem("dt_done")
        u_done = sem("u_done")
        rows_mm = sem("rows_mm")
        rows_out = sem("rows_out")
        dA_done = sem("dA_done")
        dBx_done = sem("dBx_done")
        scan_done = sem("scan_done")
        prod_done = sem("prod_done")
        ysum_done = sem("ysum_done")
        y_read = sem("y_read")
        yz_done = sem("yz_done")
        normed = sem("normed")
        scaled = sem("scaled")
        h2_done = sem("h2_done")
        xn2_done = sem("xn2_done")
        h2b_done = sem("h2b_done")
        weights_in = sem("weights_in")
        vectors_in = sem("vectors_in")
        txt_loaded = sem("txt_loaded")
        pos_in = sem("pos_in")
        top_in = sem("top_in")
        pool_prep = sem("pool_prep")
        dve_prep = sem("dve_prep")
        act_prep = sem("act_prep")
        pe_prep = sem("pe_prep")

        PRE = Step(Batch(-1), 0, scan=False, behind=False)
        FIRST = Step(Batch(0), PRE.end, behind=False)

        def odd(it):
            return Step(Batch(1, it), FIRST.end)

        def even(it):
            return Step(Batch(2, it), odd(it).end)

        LOOPS = NB // 2 - 1
        after = FIRST.end + LOOPS * 2 * len(ORDER)
        LAST = Step(Batch(NB - 1), after, ahead=False)
        POST = Step(Batch(NB), LAST.end, ahead=False, scan=False)
        assert FIRST.end % WORK == 0

        def run(eng, step):
            step(PRE)
            step(FIRST)
            with eng.Fori(0, LOOPS) as it:
                step(odd(it))
                step(even(it))
            step(LAST)
            step(POST)

        def wait_filled(eng, s, item):
            bank, uses = s.work(item)
            wait(eng, filled[bank], uses + 1)
            return work[bank]

        def wait_drained(eng, s, item):
            bank, uses = s.work(item)
            wait(eng, drained[bank], uses + 1)

        def wait_alone(eng, sem, value):
            if isinstance(value, int):
                wait(eng, sem, value)
            else:
                value = eng.to_reg(value)
                eng.wait_ge(dve_prep, ALL_DVE)
                eng.wait_ge(sem, value)

        def drained_by(s, item):
            bank, uses = s.work(item)
            return drained[bank], uses + 1

        def drains(s, item):
            return drained[s.work(item)[0]]

        E = 32
        NE = E * NTXT
        space = rings[:, :, :, :].rearrange("p a r x -> p (a r x)")
        match = space[:, 0:NE]
        place = space[:, NE:2 * NE].bitcast(I32)
        txt = obuf[:, 0, 0, 0:NTXT].bitcast(I32)
        best = xn2[:, :, 0:NTXT]
        best_i = h_post[:, 0, 0:NTXT].bitcast(I32)
        row_base = h_post[:, 1, 0:NTXT].bitcast(I32)
        rows_f = h_post[:, 2, 0:NTXT]
        none_f = x_post[:, 0, 0:NTXT]
        wx_raw = th[:, 0, 0:KD * (R + 2 * NS)].rearrange("p (k n) -> p k n", k=KD)
        pos_id = small[:, 0:2].bitcast(I32)
        alpha_e = small[:, 2:5]
        alpha_r = small[:, 5:8]
        coef = small[:, 8:17].rearrange("p (i j) -> p i j", i=3)
        half_mask = small[:, 17:18]
        ones = small[:, 18:19]
        g_cols = small[:, 20:20 + 3 * KH].rearrange("p (i m) -> p i m", i=3)
        c1 = small[:, 40:43]
        G = Bq[:, :, :, :].rearrange("p a n t -> p (a n t)")[:, 0:3 * H].rearrange("p (i h) -> p i h", i=3)
        convb = res[:, 0, :]

        block = ctx.enter_context(nc.Block())

        @block.sync
        def _(sp):
            sp.wait_ge(pool_prep, 1)
            for half in range(2):
                q = slice(64 * half, 64 * half + 64)
                sp.dma_start(txt[q, :], txt_d).then_inc(txt_loaded, 16)
                sp.dma_start(padded[q, 64 + 64 * half:64 + NTXT], txt_d[:, 0:NTXT - 64 * half]).then_inc(txt_loaded, 16)
            sp.wait_ge(dve_prep, 1)
            for b in range(2):
                sp.dma_start(img[:, b, 0:KT * NPATCH], img_d[b].rearrange("p k t -> p (k t)")).then_inc(img_in[b], 16)
            sp.dma_start(convw[:], convw_d).then_inc(weights_in, 16)
            sp.dma_start(w_in[:], win_d.rearrange("(k p) n -> p k n", k=2)).then_inc(weights_in, 16)
            sp.dma_start(wx_raw, wx_d.rearrange("(k p) n -> p k n", p=P)).then_inc(weights_in, 16)
            sp.dma_start(w_dt[:], wdt_d).then_inc(weights_in, 16)
            sp.dma_start(w_out[:], wout_d.rearrange("(k p) n -> p k n", p=P)).then_inc(weights_in, 16)
            sp.dma_start(w0[:], wfcT_d.rearrange("(k p) n -> p k n", k=2)).then_inc(weights_in, 16)
            sp.dma_start(w1[:], wprojT_d.rearrange("(k p) n -> p k n", p=P)).then_inc(weights_in, 16)
            sp.dma_start(A[:], alog_d.rearrange("(k p) n -> p k n", p=P)).then_inc(weights_in, 16)
            sp.wait_ge(dve_prep, TOPS)
            sp.dma_start(best[0:64, 1, :], best[64:128, 0, :]).then_inc(top_in, 16)

            def load(c, s, it):
                bank, uses = s.work("P1", it)
                wait(sp, filled[bank], uses + 1)
                sp.dma_start(img[:, c.par, 0:KT * NPATCH], img_d[c.index()].rearrange("p k t -> p (k t)"))\
                  .then_inc(img_in[c.par], 16)

            def store(c, s, it):
                for g in range(2):
                    bank, uses = s.work(f"G{g}", it)
                    wait(sp, drained[bank], uses + 1)
                sp.dma_start(out_d[c.index(), 0:NPATCH, :].rearrange("(t p) c -> p t c", p=TP),
                             obuf[0:TP, c.par, 0:2, :]).then_inc(out_stored[c.par], 16)
                sp.dma_start(out_d[c.index(), NPATCH:NTOK, :], obuf[:, c.par, 2, :])\
                  .then_inc(out_stored[c.par], 16)

            load(Batch(2), PRE, None)
            load(Batch(3), FIRST, None)
            with sp.Fori(0, NB // 2 - 2) as it:
                for o in range(2):
                    s = (odd, even)[o](it)
                    store(Batch(o, it), s, it)
                    wait_alone(sp, out_stored[o], it * 32 + 32)
                    load(Batch(4 + o, it), s, it)
            for b in range(NB - 4, NB - 2):
                it = b // 2
                s = (odd, even)[b % 2](0)
                store(Batch(b), s, it)
            store(Batch(NB - 2), LAST, None)
            store(Batch(NB - 1), POST, None)
            for q in range(2):
                sp.wait_ge(out_stored[q], 32 * (NB // 2))

        @block.gpsimd
        def _(pool):
            prep = [0]

            def link(ins):
                ins.then_inc(pool_prep, 1)
                prep[0] += 1
                pool.wait_ge(pool_prep, prep[0])

            link(nc.gpsimd.memset(padded[:], -1))
            pool.dma_start(pos_id[0:TP, :], posid_d).then_inc(pos_in, 16)
            for dst, src in ((alpha_e, ae_d), (alpha_r, ar_d), (gamma[:], gamma_d), (beta[:], beta_d),
                             (b1[:], bproj_d), (convb, convb_d)):
                pool.dma_start(dst, src.partition_broadcast(P)).then_inc(vectors_in, 16)
            for dst, src in ((b_dt, bdt_d), (d_half, dskip_d), (b0, bfc_d)):
                pool.dma_start(dst[:], src).then_inc(vectors_in, 16)
            link(nc.gpsimd.iota(place[0:64, :], pattern=[[1, E], [1, NTXT]], base=-64, channel_multiplier=0))
            link(nc.gpsimd.iota(place[64:128, :], pattern=[[1, E], [1, NTXT]], base=-128, channel_multiplier=0))
            link(nc.gpsimd.iota(row_base[0:64, :], pattern=[[0, NTXT]], base=1, channel_multiplier=NTXT))
            link(nc.gpsimd.memset(ident[:], 0.0))
            link(nc.gpsimd.affine_select(out=ident[:], in_=ident[:], compare_op=ALU.not_equal, fill=1.0, base=0,
                                         pattern=[[-1, P]], channel_multiplier=1))
            link(nc.gpsimd.memset(row_sel[:], 0.0))
            for part in range(3):
                link(nc.gpsimd.affine_select(out=row_sel[:], in_=row_sel[:], compare_op=ALU.not_equal, fill=1.0,
                                             base=-2 * NS * part, pattern=[[-1, 2 * NS], [0, P]],
                                             channel_multiplier=1))
            link(nc.gpsimd.memset(ones, 1.0))
            link(nc.gpsimd.memset(half_mask, 1.0))
            link(nc.gpsimd.affine_select(out=half_mask, in_=half_mask, compare_op=ALU.is_ge, fill=0.0,
                                         base=EMBED_CHOICES[1] - CH - 1, pattern=[[0, 1]], channel_multiplier=-1))
            link(nc.gpsimd.memset(minus_half[:], -0.5))
            link(nc.gpsimd.memset(pos[:], 0.0))
            assert prep[0] == POOL_CONST
            pool.wait_ge(pos_in, 16)
            for t in range(2):
                pool.indirect_dma_start(pos[0:TP, t, :], None, pos_d, bass.IndirectOffsetOnAxis(
                    ap=pos_id[0:TP, t:t + 1], axis=0)).then_inc(pos_in, 16)
            pool.wait_ge(dve_prep, CHUNK0)
            link(nc.gpsimd.iota(place[0:64, :], pattern=[[1, E], [1, NTXT]], base=E - 64, channel_multiplier=0))
            link(nc.gpsimd.iota(place[64:128, :], pattern=[[1, E], [1, NTXT]], base=E - 128, channel_multiplier=0))
            pool.wait_ge(dve_prep, ALL_DVE)

            def unit(s, j):
                b, q, r = s.batch, j // KD, j % RING
                pool.wait_ge(scan_done, b.count(UNITS, j + 1))
                if j % KD == 0:
                    pool.wait_ge(rows_out, b.count(PAIRS, 4 * q + 4))
                nc.gpsimd.tensor_tensor(st[:, r], st[:, r], Cq[:, q % 2], ALU.mult).then_inc(prod_done, 1)

            def norm(b, which):
                wait_alone(pool, mv_done[which], b.count(3, 3))
                nc.gpsimd.tensor_scalar(veps[:, which, :], mv[:, which, :, 1], EPS, None, ALU.add)\
                    .then_inc(veps_done[which], 1)
                pool.wait_ge(veps_done[which], b.count(1, 1))
                nc.gpsimd.tensor_tensor(rstd[:, which, :], veps[:, which, :], minus_half[:], ALU.pow)\
                    .then_inc(rstd_done[which], 1)

            def step(s):
                a, c = s.batch.plus(1), s.batch.plus(-1)
                for j in range(UNITS):
                    if j == 0 and s.behind:
                        wait(pool, xn_done, c.count(3, 3))
                        nc.gpsimd.tensor_tensor(h_post[:], h[:, c.par], beta[:, None, :].broadcast_to([P, 3, C]),
                                                ALU.add).then_inc(posted, 1)
                        nc.gpsimd.tensor_copy(x_post[:], xn[:, c.par]).then_inc(posted, 1)
                    if j == 0 and s.ahead:
                        wait_alone(pool, txt_copied, a.count(1, 0))
                        nc.gpsimd.tensor_copy(txt_row[:], row_table[:, bass.ds(a.index(), 1)]).then_inc(row_ready, 1)
                        nc.gpsimd.memset(txt_tok[:], NO_ROW).then_inc(row_ready, 1)
                        nc.gpsimd.memset(txt_emb[:], 0.0).then_inc(row_ready, 1)
                        wait_alone(pool, row_ready, a.count(3, 3))
                        pool.indirect_dma_start(txt_tok[:], None, txt_d.rearrange("b (t o) -> (b t) o", o=1),
                                                bass.IndirectOffsetOnAxis(ap=txt_row[:, 0:1], axis=0),
                                                bounds_check=NB * NTXT - 1, oob_is_err=False).then_inc(tok_in, 16)
                    if j == 2 and s.ahead:
                        norm(a, 0)
                    if j == 3 and s.behind:
                        norm(c, 1)
                    if j == 4 and s.behind:
                        norm(c, 2)
                    if j == 5 and s.behind:
                        pool.wait_ge(h2_done, c.count(1, 1))
                        nc.gpsimd.tensor_tensor(h_post[:], res[:], b1[:, None, :].broadcast_to([P, 3, C]),
                                                ALU.add).then_inc(h2b_done, 1)
                    if j == 8 and s.ahead:
                        if s.scan:
                            pool.wait_ge(prod_done, s.batch.count(UNITS, j))
                        wait_alone(pool, *drained_by(s, "X1"))
                        nc.gpsimd.tensor_copy(bc3[32:64, a.par], bc_rest[32:64, :]).then_inc(bc_lo, 1)
                        nc.gpsimd.tensor_copy(bc_mid[64:96, :], bc_rest[64:96, :]).then_inc(bc_q, 1)
                        pool.wait_ge(bc_q, a.count(1, 1))
                        nc.gpsimd.tensor_tensor(bc3[64:96, a.par], bc_rest[64:96, :], bc_mid[64:96, :],
                                                ALU.subtract).then_inc(bc_lo, 1)
                        pool.wait_ge(bc_lo, a.count(2, 2))
                    if j == 9 and s.ahead:
                        wait_alone(pool, sp_act, a.count(3, 2))
                        nc.gpsimd.tensor_scalar(corr[:], th[:, KD:2 * KD], 1.0, None, ALU.subtract)\
                            .then_inc(sp_pool, 1)
                        pool.wait_ge(sp_pool, a.count(3, 1))
                        nc.gpsimd.tensor_tensor(corr[:], corr[:], th[:, 0:KD], ALU.subtract).then_inc(sp_pool, 1)
                        pool.wait_ge(sp_pool, a.count(3, 2))
                        wait_drained(pool, s, "D2")
                        nc.gpsimd.tensor_tensor(corr[:], relu[:], corr[:], ALU.subtract).then_inc(sp_pool, 1)
                    if s.scan:
                        unit(s, j)
                    if j == 0 and s.ahead:
                        wait_alone(pool, tok_in, a.count(16, 16))
                        pool.indirect_dma_start(txt_emb[:], None, emb_d,
                                                bass.IndirectOffsetOnAxis(ap=txt_tok[:, 0:1], axis=0),
                                                bounds_check=V - 1, oob_is_err=False).then_inc(emb_in, 16)
                    if j == 1 and s.ahead:
                        pool.wait_ge(emb_in, a.count(16, 16))
                        wait_alone(pool, posted, a.plus(-2).count(2, 2))
                        nc.gpsimd.tensor_copy(h[:, a.par, 2, :], txt_emb[:]).then_inc(txt_copied, 1)

            run(pool, step)

        @block.scalar
        def _(act):
            act.wait_ge(weights_in, WEIGHTS)
            act.wait_ge(vectors_in, VECTORS)
            nc.scalar.activation(A[:], A[:], ACT.Exp).then_inc(act_prep, 1)
            act.wait_ge(act_prep, 1)
            nc.scalar.activation(A[:], A[:], ACT.Copy, scale=-1.0).then_inc(act_prep, 1)
            nc.scalar.activation(w_dt_rows[:], wx_raw[:, :, 0:R], ACT.Copy, scale=0.5).then_inc(act_prep, 1)
            for part in range(3):
                nc.scalar.activation(w_bc[:, :, part, :], wx_raw[:, :, R:R + 2 * NS], ACT.Copy, scale=0.5)\
                    .then_inc(act_prep, 1)
            nc.scalar.activation(w_out[:], w_out[:], ACT.Copy, scale=0.5).then_inc(act_prep, 1)
            act.wait_ge(act_prep, 7)
            act.wait_ge(dve_prep, ALL_DVE)

            def decay(b, j):
                q, k, r = j // KD, j % KD, j % RING
                if j == 0:
                    act.wait_ge(dt_done, b.count(1, 1))
                wait(act, scan_done, b.count(UNITS, j + 1 - RING))
                for i in range(QS):
                    n = q * QS + i
                    last = nc.scalar.activation(dA[:, r, i, 1:NTOK], dt[:, b.par, k, 1:NTOK], ACT.Exp,
                                                scale=A[:, k, n:n + 1])
                last.then_inc(dA_done, 1)

            def rows(b, pair):
                q, kind, half = pair // 4, pair % 4 // 2, pair % 2
                act.wait_ge(rows_mm, b.count(PAIRS, pair + 1))
                wait(act, (dBx_done, prod_done)[kind], b.count(UNITS, KD * (q - 1)))
                dst = (Bq, Cq)[kind]
                nc.scalar.activation(dst[:, q % 2, 2 * half:2 * half + 2, :], row_ps[:, :, 0:NTOK], ACT.Copy)\
                    .then_inc(rows_out, 1)

            def quad_rows(s, j):
                q = j // KD + 1
                b = s.batch if q < NQ else s.batch.plus(1)
                if (s.scan if q < NQ else s.ahead):
                    for pair in ((0,), (1, 2), (3,))[j % KD]:
                        rows(b, 4 * (q % NQ) + pair)

            def step(s):
                a, c = s.batch.plus(1), s.batch.plus(-1)
                for j in range(UNITS):
                    if s.scan:
                        for n in DECAYS.get(j, ()):
                            decay(s.batch, n)
                    if j == 3 and s.ahead:
                        for k in range(2):
                            bank = wait_filled(act, s, f"T{k}")
                            nc.scalar.activation(xT[:, k, :], bank[0:CH, 0:NTOK], ACT.Copy)\
                                .then_inc(drains(s, f"T{k}"), 1)
                    if j == 5 and s.ahead:
                        wait(act, sp_pool, a.count(3, 0))
                        for m in range(2 * KD):
                            bank = wait_filled(act, s, f"M{m}")
                            nc.scalar.activation(th[:, m, :], bank[:, 0:NTOK], ACT.Tanh, scale=0.5)\
                                .then_inc(th_done, 1)
                    if j == 5 and s.behind:
                        for k in range(2):
                            bank = wait_filled(act, s, f"U{k}")
                            nc.scalar.activation(x2T[:, k, :], bank[0:CH, 0:NTOK], ACT.Copy)\
                                .then_inc(drains(s, f"U{k}"), 1)
                    if j == 6 and s.behind:
                        for m in range(KH):
                            bank = wait_filled(act, s, f"F{m}")
                            nc.scalar.activation(gT[:, m, :], bank[:, 0:NTOK], ACT.Gelu_apprx_tanh,
                                                 bias=b0[:, m:m + 1]).then_inc(drains(s, f"F{m}"), 1)
                    if j == 7 and s.ahead:
                        bank = wait_filled(act, s, "X0")
                        nc.scalar.activation(dt_rows[:], bank[0:R, 0:NTOK], ACT.Copy).then_inc(drains(s, "X0"), 1)
                        bank = wait_filled(act, s, "X1")
                        nc.scalar.activation(bc3[:, a.par], bank[0:96, 0:NTOK], ACT.Copy).then_inc(bc_hi, 1)
                    if j == 8 and s.ahead:
                        for k in range(KD):
                            bank = wait_filled(act, s, f"D{k}")
                            nc.scalar.activation(th[:, k, :], bank[:, 0:NTOK], ACT.Abs, bias=b_dt[:, k:k + 1])\
                                .then_inc(abs_done, 1)
                        act.wait_ge(abs_done, a.count(3, 3))
                        nc.scalar.activation(th[:, 0:KD], th[:, 0:KD], ACT.Exp, scale=-1.0).then_inc(sp_act, 1)
                        act.wait_ge(sp_act, a.count(3, 1))
                        wait_drained(act, s, f"M{2 * KD - 1}")
                        nc.scalar.activation(th[:, KD:2 * KD], th[:, 0:KD], ACT.Identity, bias=1.0)\
                            .then_inc(sp_act, 1)
                        act.wait_ge(sp_act, a.count(3, 2))
                        nc.scalar.activation(dt[:, a.par], th[:, KD:2 * KD], ACT.Ln).then_inc(sp_act, 1)
                    quad_rows(s, j)
                if s.ahead:
                    decay(a, 0)

            run(act, step)

        @block.tensor
        def _(pe):
            pe.wait_ge(dve_prep, G_READY)
            pe.wait_ge(pool_prep, POOL_CONST)
            for i in range(3):
                for m in range(KH):
                    last = nc.tensor.matmul(work[0][:, i * KH + m:i * KH + m + 1], G[0:1, i, m * P:(m + 1) * P],
                                            ones[0:1, :], start=True, stop=True)
            last.then_inc(pe_prep, 1)
            pe.wait_ge(dve_prep, ROWS_READY)
            nc.tensor.transpose(work[1][:, 0:64], rows_f[0:64, :], ident[0:64, 0:64]).then_inc(pe_prep, 1)
            pe.wait_ge(act_prep, 7)
            pe.wait_ge(dve_prep, ALL_DVE)

            def begin(s, item):
                bank, uses = s.work(item)
                wait(pe, drained[bank], uses)
                return work[bank], filled[bank]

            def ysum(b, j):
                q, k, r = j // KD, j % KD, j % RING
                pe.wait_ge(prod_done, b.count(UNITS, j + 1))
                if q == 0:
                    wait(pe, y_read, b.count(KD, k + 1 - KD))
                for i in range(QS):
                    last = nc.tensor.matmul(y_ps[:, k, 0:NTOK], ident[:], st[:, r, i, :],
                                            start=(q == 0 and i == 0), stop=(q == NQ - 1 and i == QS - 1))
                last.then_inc(ysum_done, 1)

            def rows(b, pair):
                q, kind, half = pair // 4, pair % 4 // 2, pair % 2
                if pair == 0:
                    pe.wait_ge(bc_hi, b.count(1, 1))
                    pe.wait_ge(bc_lo, b.count(2, 2))
                wait(pe, rows_out, b.count(PAIRS, pair))
                for i in range(2):
                    n = kind * NS + q * QS + 2 * half + i
                    last = nc.tensor.matmul(row_ps[:, i, 0:NTOK], row_sel[:, n, :], bc3[:, b.par, :],
                                            start=True, stop=True)
                last.then_inc(rows_mm, 1)

            def quad_rows(s, j):
                q = j // KD + 1
                b = s.batch if q < NQ else s.batch.plus(1)
                if (s.scan if q < NQ else s.ahead):
                    for pair in ((0,), (1, 2), (3,))[j % KD]:
                        rows(b, 4 * (q % NQ) + pair)

            def step(s):
                a, c = s.batch.plus(1), s.batch.plus(-1)

                def project(names, weights, x, width):
                    for m in names:
                        bank, full = begin(s, f"{width}{m}")
                        for k in range(2):
                            last = nc.tensor.matmul(bank[:, 0:NTOK], weights[:, k, m * P:(m + 1) * P], x[:, k, :],
                                                    start=(k == 0), stop=(k == 1))
                        last.then_inc(full, 1)

                def turn(item, x):
                    for k in range(2):
                        bank, full = begin(s, f"{item}{k}")
                        for t, (t0, n) in enumerate(TOK):
                            last = nc.tensor.transpose(bank[0:CH, t0:t0 + n], x[0:n, t, k * CH:(k + 1) * CH],
                                                       ident[0:n, 0:n])
                        last.then_inc(full, 1)

                def to_tokens(item, x, weights, n):
                    for g, tiles in enumerate(((0, 1), (2,))):
                        bank, full = begin(s, f"{item}{g}")
                        for i, t in enumerate(tiles):
                            t0 = TOK[t][0]
                            for k in range(n):
                                last = nc.tensor.matmul(bank[:, i * C:(i + 1) * C], x[:, k, t0:t0 + P],
                                                        weights[:, k, :], start=(k == 0), stop=(k == n - 1))
                        last.then_inc(full, 1)

                for j in range(UNITS):
                    if j == 0 and s.behind:
                        ysum(c, UNITS - 1)
                    if j == 1 and s.ahead:
                        pe.wait_ge(img_in[a.par], a.plus(2).pair_count(16))
                        for t in range(2):
                            bank, full = begin(s, f"P{t}")
                            for k in range(KT):
                                t0 = k * NPATCH + t * TP
                                last = nc.tensor.matmul(bank[:, 0:C], img[:, a.par, t0:t0 + P], convw[:, k, :],
                                                        start=(k == 0), stop=(k == KT - 1))
                            last.then_inc(full, 1)
                    if j == 2 and s.behind:
                        pe.wait_ge(yz_done, c.count(1, 1))
                        to_tokens("O", yz, w_out, KD)
                    if j == 3 and s.ahead:
                        pe.wait_ge(xn_done, a.count(3, 3))
                        turn("T", xn[:, a.par])
                    if j == 4 and s.ahead:
                        wait_drained(pe, s, "T1")
                        project(range(0, 3), w_in, xT, "M")
                    if j == 5 and s.ahead:
                        project(range(3, 6), w_in, xT, "M")
                    if j == 5 and s.behind:
                        pe.wait_ge(xn2_done, c.count(3, 3))
                        turn("U", xn2)
                    if j == 6 and s.behind:
                        wait_drained(pe, s, "U1")
                        project(range(0, 3), w0, x2T, "F")
                    if j == 7 and s.behind:
                        project(range(3, 6), w0, x2T, "F")
                    if j == 7 and s.ahead:
                        wait_drained(pe, s, "M2")
                        bank, full = begin(s, "X0")
                        for k in range(KD):
                            last = nc.tensor.matmul(bank[0:R, 0:NTOK], w_dt_rows[:, k, :], xz[:, a.par, k, :],
                                                    start=(k == 0), stop=(k == KD - 1))
                        last.then_inc(full, 1)
                        bank, full = begin(s, "X1")
                        for k in range(KD):
                            last = nc.tensor.matmul(bank[0:96, 0:NTOK], w_bc[:, k, :, :].rearrange("p a n -> p (a n)"),
                                                    xz[:, a.par, k, :], start=(k == 0), stop=(k == KD - 1))
                        last.then_inc(full, 1)
                    if j == 8 and s.ahead:
                        wait_drained(pe, s, "X0")
                        for k in range(KD):
                            bank, full = begin(s, f"D{k}")
                            nc.tensor.matmul(bank[:, 0:NTOK], w_dt[:, k * P:(k + 1) * P], dt_rows[:],
                                             start=True, stop=True).then_inc(full, 1)
                    if j == 9 and s.behind:
                        wait_drained(pe, s, "F5")
                        to_tokens("G", gT, w1, KH)
                    quad_rows(s, j)
                    if s.scan and j >= 1:
                        ysum(s.batch, j - 1)

            run(pe, step)

        @block.vector
        def _(dve):
            prep = [0]

            def link(ins):
                ins.then_inc(dve_prep, 1)
                prep[0] += 1
                dve.wait_ge(dve_prep, prep[0])

            link(nc.vector.memset(img[:], 0.0))
            dve.wait_ge(weights_in, WEIGHTS)
            dve.wait_ge(vectors_in, VECTORS)
            dve.wait_ge(pool_prep, POOL_CONST)
            for i in range(3):
                link(nc.vector.tensor_scalar(coef[:, i, :], alpha_r, alpha_e[:, i:i + 1], None, ALU.mult))
            link(nc.vector.memset(G, 0.0))
            for i, e in enumerate(EMBED_CHOICES):
                for j, r in enumerate(RATIO_CHOICES):
                    link(nc.vector.tensor_scalar(G[:, i, 0:r * e], G[:, i, 0:r * e], coef[:, i, j:j + 1], None,
                                                 ALU.add))
            assert prep[0] == G_READY
            scr = gT[:, :, :].rearrange("p m t -> p (m t)")[:, 0:H]
            link(nc.vector.scalar_tensor_tensor(scr[0:CH, :], G[0:CH, 1, :], half_mask[0:CH, :], G[0:CH, 2, :],
                                                ALU.mult, ALU.add))
            link(nc.vector.tensor_tensor(w0[:, 1, :], w0[:, 1, :], scr[0:CH, :], ALU.mult))
            link(nc.vector.tensor_tensor(scr[0:CH, :], G[0:CH, 0, :], G[0:CH, 1, :], ALU.add))
            link(nc.vector.tensor_tensor(scr[0:CH, :], scr[0:CH, :], G[0:CH, 2, :], ALU.add))
            link(nc.vector.tensor_tensor(w0[:, 0, :], w0[:, 0, :], scr[0:CH, :], ALU.mult))
            dve.wait_ge(pe_prep, 1)
            link(nc.vector.tensor_copy(g_cols, work[0][:, 0:3 * KH].rearrange("p (i m) -> p i m", i=3)))
            for i in (1, 0):
                link(nc.vector.tensor_tensor(g_cols[:, i, :], g_cols[:, i, :], g_cols[:, i + 1, :], ALU.add))
            link(nc.vector.tensor_tensor(b0[:], b0[:], g_cols[:, 0, :], ALU.mult))
            link(nc.vector.tensor_reduce(c1, coef, AX.X, ALU.add))
            for i in (1, 0):
                link(nc.vector.tensor_tensor(c1[:, i:i + 1], c1[:, i:i + 1], c1[:, i + 1:i + 2], ALU.add))
            lo = 0
            for i, e in enumerate(EMBED_CHOICES):
                link(nc.vector.tensor_tensor(w1[:, :, lo:e], w1[:, :, lo:e],
                                             g_cols[:, i, :, None].broadcast_to([P, KH, e - lo]), ALU.mult))
                link(nc.vector.tensor_scalar(b1[:, lo:e], b1[:, lo:e], c1[:, i:i + 1], None, ALU.mult))
                lo = e
            link(nc.vector.tensor_scalar(d_half[:], d_half[:], 0.5, None, ALU.mult))
            dve.wait_ge(pos_in, 48)
            link(nc.vector.tensor_tensor(pos[:], pos[:], convb[:, None, :].broadcast_to([P, 2, C]), ALU.add))

            dve.wait_ge(txt_loaded, 64)
            for chunk in range(2):
                shifted = padded[:, chunk * E:chunk * E + NTXT]
                shifted = bass.AP(tensor=shifted.tensor, offset=shifted.offset,
                                  ap=[shifted.ap[0], [1, E], [1, NTXT]])
                m3 = match.rearrange("p (e i) -> p e i", e=E)
                link(nc.vector.tensor_tensor(m3, txt[:, None, :].broadcast_to([P, E, NTXT]), shifted, ALU.is_equal))
                link(nc.vector.tensor_tensor_scan(match, match, match, 0.0, ALU.mult, ALU.add))
                if chunk == 1:
                    dve.wait_ge(pool_prep, POOL_CONST + 2)
                link(nc.vector.scalar_tensor_tensor(match, match, float(NTXT), place, ALU.mult, ALU.add))
                link(nc.vector.tensor_reduce(best[:, chunk, :], match.rearrange("p (e i) -> p i e", e=E), AX.X,
                                             ALU.max))
                if chunk == 0:
                    assert prep[0] == CHUNK0
            link(nc.vector.tensor_tensor(best[:, 0, :], best[:, 0, :], best[:, 1, :], ALU.max))
            assert prep[0] == TOPS
            dve.wait_ge(top_in, 16)
            low = slice(0, 64)
            link(nc.vector.tensor_tensor(best[low, 0, :], best[low, 0, :], best[low, 1, :], ALU.max))
            link(nc.vector.tensor_copy(best_i[low, :], best[low, 0, :]))
            link(nc.vector.tensor_scalar(best_i[low, :], best_i[low, :], NTXT - 1, None, ALU.bitwise_and))
            link(nc.vector.tensor_tensor(rows_f[low, :], best_i[low, :], row_base[low, :], ALU.add))
            link(nc.vector.tensor_scalar(none_f[low, :], best[low, 0, :], float(NTXT), float(NO_ROW), ALU.is_lt,
                                         ALU.mult))
            link(nc.vector.tensor_tensor(rows_f[low, :], rows_f[low, :], none_f[low, :], ALU.add))
            assert prep[0] == ROWS_READY
            dve.wait_ge(pe_prep, 2)
            link(nc.vector.tensor_copy(row_table[:], work[1][:, 0:64]))
            link(nc.vector.memset(dA[:, :, :, 0:1], 0.0))
            assert prep[0] == ALL_DVE

            def normalise(b, which, x, out, done):
                dve.wait_ge(rstd_done[which], b.count(1, 1))
                for t in range(3):
                    nc.vector.tensor_scalar(out[:, t, :], x[:, t, :], mv[:, which, t, 0:1],
                                            rstd[:, which, t:t + 1], ALU.subtract, ALU.mult).then_inc(done, 1)

            def moments(b, which, x):
                for t in range(3):
                    nc.vector.bn_stats(stats[:, which, t, :], x[:, t, :]).then_inc(stat_done[which], 1)
                wait_alone(dve, stat_done[which], b.count(3, 3))
                for t in range(3):
                    nc.vector.bn_aggr(mv[:, which, t, :], stats[:, which, t, :]).then_inc(mv_done[which], 1)

            def drive(b, j):
                q, k, r = j // KD, j % KD, j % RING
                if j == 0:
                    dve.wait_ge(u_done, b.count(1, 1))
                if k == 0:
                    dve.wait_ge(rows_out, b.count(PAIRS, 4 * q + 2))
                wait(dve, ysum_done, b.count(UNITS, j + 1 - RING))
                nc.vector.tensor_tensor(st[:, r], u[:, b.par, k, None, :].broadcast_to([P, QS, NTOK]), Bq[:, q % 2],
                                        ALU.mult).then_inc(dBx_done, 1)

            def scan(b, j):
                r = j % RING
                dve.wait_ge(dA_done, b.count(UNITS, j + 1))
                dve.wait_ge(dBx_done, b.count(UNITS, j + 1))
                nc.vector.tensor_tensor_scan(rings[:, 1, r, :], rings[:, 0, r, :], rings[:, 1, r, :], 0.0,
                                             ALU.mult, ALU.add).then_inc(scan_done, 1)

            def step(s):
                a, c = s.batch.plus(1), s.batch.plus(-1)

                def gate(names):
                    for m in names:
                        bank = wait_filled(dve, s, f"M{m}")
                        dve.wait_ge(th_done, a.count(6, m + 1))
                        nc.vector.scalar_tensor_tensor(xz[:, a.par, m, :], th[:, m, :], 1.0, bank[:, 0:NTOK],
                                                       ALU.add, ALU.mult).then_inc(drains(s, f"M{m}"), 1)

                for j in range(UNITS):
                    if j == 1 and s.behind:
                        for k in range(KD):
                            dve.wait_ge(ysum_done, c.count(UNITS, UNITS - KD + k + 1))
                            nc.vector.scalar_tensor_tensor(yz[:, k, :], xz[:, c.par, k, :], d_half[:, k:k + 1],
                                                           y_ps[:, k, 0:NTOK], ALU.mult, ALU.add).then_inc(y_read, 1)
                        dve.wait_ge(y_read, c.count(KD, KD))
                        nc.vector.tensor_tensor(yz[:], yz[:], xz[:, c.par, KD:2 * KD], ALU.mult)\
                            .then_inc(yz_done, 1)
                    if j == 2 and s.ahead:
                        wait(dve, posted, a.plus(-2).count(2, 2))
                        for t in range(2):
                            bank = wait_filled(dve, s, f"P{t}")
                            nc.vector.tensor_tensor(h[:, a.par, t, :], bank[:, 0:C], pos[:, t, :], ALU.add)\
                                .then_inc(drains(s, f"P{t}"), 1)
                        wait_drained(dve, s, "P0")
                        wait_drained(dve, s, "P1")
                        dve.wait_ge(txt_copied, a.count(1, 1))
                        moments(a, 0, h[:, a.par])
                    if j == 3 and s.ahead:
                        dve.wait_ge(mv_done[0], a.count(3, 3))
                        normalise(a, 0, h[:, a.par], xn[:, a.par], xn_done)
                    if j == 3 and s.behind:
                        dve.wait_ge(posted, c.count(2, 2))
                        for g, (t0, t1) in enumerate(((0, 2), (2, 3))):
                            bank = wait_filled(dve, s, f"O{g}")
                            nc.vector.tensor_tensor(res[:, t0:t1, :],
                                                    bank[:, 0:(t1 - t0) * C].rearrange("p (t c) -> p t c", c=C),
                                                    x_post[:, t0:t1, :], ALU.add).then_inc(drains(s, f"O{g}"), 1)
                        wait_drained(dve, s, "O0")
                        wait_drained(dve, s, "O1")
                        moments(c, 1, res)
                    if j == 4 and s.behind:
                        normalise(c, 1, res, res, normed)
                        dve.wait_ge(normed, c.count(3, 3))
                        nc.vector.tensor_tensor(res[:], res[:], gamma[:, None, :].broadcast_to([P, 3, C]), ALU.mult)\
                            .then_inc(scaled, 1)
                        dve.wait_ge(scaled, c.count(1, 1))
                        nc.vector.tensor_tensor(res[:], res[:], h_post[:], ALU.add).then_inc(h2_done, 1)
                        dve.wait_ge(h2_done, c.count(1, 1))
                        moments(c, 2, res)
                    if j == 5 and s.behind:
                        normalise(c, 2, res, xn2, xn2_done)
                    if j == 5 and s.ahead:
                        gate(range(0, 3))
                    if j == 6 and s.ahead:
                        gate(range(3, 6))
                    if j == 8 and s.ahead:
                        wait_filled(dve, s, "X1")
                        dve.wait_ge(bc_hi, a.count(1, 1))
                        wait(dve, bc_lo, a.count(2, 0))
                        bank = work[s.work("X1")[0]]
                        nc.vector.tensor_tensor(bc_rest[:], bank[0:96, 0:NTOK], bc3[:, a.par], ALU.subtract)\
                            .then_inc(drains(s, "X1"), 1)
                    if j == 9 and s.ahead:
                        for k in range(KD):
                            bank = wait_filled(dve, s, f"D{k}")
                            dve.wait_ge(abs_done, a.count(3, k + 1))
                            nc.vector.tensor_scalar(relu[:, k, :], bank[:, 0:NTOK], b_dt[:, k:k + 1], 0.0, ALU.add,
                                                    ALU.max).then_inc(drains(s, f"D{k}"), 1)
                    if j == 10 and s.ahead:
                        dve.wait_ge(sp_act, a.count(3, 3))
                        dve.wait_ge(sp_pool, a.count(3, 3))
                        nc.vector.tensor_tensor(dt[:, a.par], dt[:, a.par], corr[:], ALU.add).then_inc(dt_done, 1)
                        dve.wait_ge(dt_done, a.count(1, 1))
                        nc.vector.scalar_tensor_tensor(u[:, a.par], xz[:, a.par, 0:KD], 0.5, dt[:, a.par], ALU.mult,
                                                       ALU.mult).then_inc(u_done, 1)
                    if j == 10 and s.behind:
                        if c.it is None:
                            wait(dve, out_stored[c.par], c.pair_count(32))
                        dve.wait_ge(h2b_done, c.count(1, 1))
                        for g, (t0, t1) in enumerate(((0, 2), (2, 3))):
                            bank = wait_filled(dve, s, f"G{g}")
                            nc.vector.tensor_tensor(obuf[:, c.par, t0:t1, :],
                                                    bank[:, 0:(t1 - t0) * C].rearrange("p (t c) -> p t c", c=C),
                                                    h_post[:, t0:t1, :], ALU.add).then_inc(drains(s, f"G{g}"), 1)
                    if s.scan:
                        if j + 1 < UNITS:
                            drive(s.batch, j + 1)
                        elif s.ahead:
                            drive(a, 0)
                        scan(s.batch, j)
                    elif s.ahead and j == UNITS - 1:
                        drive(a, 0)

            run(dve, step)


WEIGHTS = 16 * 8
VECTORS = 16 * (6 + 3)
POOL_CONST = 15
G_READY = 1 + 3 + 1 + 9
CHUNK0 = G_READY + 5 + 1 + 2 + 1 + 1 + 2 + 6 + 1 + 1 + 4
TOPS = CHUNK0 + 4 + 1
ROWS_READY = TOPS + 6
ALL_DVE = ROWS_READY + 2
DECAYS = {0: (1,), 1: (2,), 2: (3,), 3: (4,), 4: (5, 6, 7), 7: (8,), 8: (9,), 9: (10,), 10: (11,)}


def kernel(x, x_txt, L0_tok_conv_w, L0_tok_conv_b, L0_tok_pos_table, L0_txt_emb, L0_attn_W_in, L0_attn_W_x,
           L0_attn_W_dt, L0_attn_b_dt, L0_attn_A_log, L0_attn_D_skip, L0_attn_W_out, L0_attn_gamma, L0_attn_beta,
           L0_ffn_w_fc, L0_ffn_b_fc, L0_ffn_w_proj, L0_ffn_b_proj, L0_ffn_alpha_e, L0_ffn_alpha_r):
    import numpy as np
    import concourse.bacc as bacc
    from concourse.bass_utils import run_bass_kernel_spmd

    NB, CI, HW, _ = x.shape
    C = L0_tok_conv_w.shape[0]
    NT = x_txt.shape[1]
    side = HW // PATCH
    grid = int(round(L0_tok_pos_table.shape[0] ** 0.5))
    kt = CI * PATCH * PATCH // P
    img = np.asarray(x).reshape(NB, CI, side, PATCH, side, PATCH).transpose(0, 1, 3, 5, 2, 4)
    img = img.reshape(NB, kt, P, side * side).transpose(0, 2, 1, 3)
    convw = np.asarray(L0_tok_conv_w).reshape(C, kt, P).transpose(2, 1, 0)
    edges = np.arange(1.0 / grid, 1.0, 1.0 / grid, dtype=np.float32)
    frac = np.arange(0.0, 1.0 - 1e-06, 1.0 / side, dtype=np.float32)
    bucket = np.searchsorted(edges, frac, side="right")
    pos_id = (bucket[:, None] * grid + bucket).reshape(2, -1).T.astype(np.int32)

    arrays = {
        "img": img, "txt": x_txt, "convw": convw, "convb": L0_tok_conv_b, "pos": L0_tok_pos_table, "pos_id": pos_id,
        "emb": L0_txt_emb, "w_in": L0_attn_W_in, "w_x": L0_attn_W_x, "w_dt": L0_attn_W_dt, "b_dt": np.asarray(L0_attn_b_dt).reshape(-1, P).T,
        "a_log": L0_attn_A_log, "d_skip": np.asarray(L0_attn_D_skip).reshape(-1, P).T, "w_out": L0_attn_W_out, "gamma": L0_attn_gamma,
        "beta": L0_attn_beta, "w_fc_t": np.asarray(L0_ffn_w_fc).T, "b_fc": np.asarray(L0_ffn_b_fc).reshape(-1, P).T,
        "w_proj_t": np.asarray(L0_ffn_w_proj).T, "b_proj": L0_ffn_b_proj, "alpha_e": L0_ffn_alpha_e,
        "alpha_r": L0_ffn_alpha_r,
    }
    arrays = {k + "_dram": np.ascontiguousarray(v) for k, v in arrays.items()}
    nc = bacc.Bacc("TRN2", target_bir_lowering=False, num_devices=1)
    args = [nc.dram_tensor(k, v.shape, mybir.dt.from_np(v.dtype), kind="ExternalInput").ap() for k, v in arrays.items()]
    out = nc.dram_tensor("out_dram", (NB, side * side + NT, C), F32, kind="ExternalOutput").ap()
    build(nc, *args, out)
    r = run_bass_kernel_spmd(nc, [arrays], core_ids=[0])
    return r.results[0]["out_dram"]
```

```python
from contextlib import ExitStack

import concourse.bass as bass
from concourse import mybir

F32 = mybir.dt.float32
BF16 = mybir.dt.bfloat16
I32 = mybir.dt.int32
ALU = mybir.AluOpType
ACT = mybir.ActivationFunctionType
AX = mybir.AxisListType

P = 128
BANK = 512
PATCH = 16
EPS = 1e-5
EMBED_CHOICES = (96, 144, 192)
RATIO_CHOICES = (2, 3, 4)
NO_ROW = 1 << 20

AHEAD = {"P": 2, "T": 2, "M": 6, "X": 2, "D": 3}
BEHIND = {"O": 2, "U": 2, "F": 6, "G": 2}
ORDER = (["P0", "P1", "T0", "T1", "O0", "O1"] + [f"M{m}" for m in range(6)] + ["X0", "X1", "U0", "U1"]
         + ["D0", "D1", "D2"] + [f"F{m}" for m in range(6)] + ["G0", "G1"])
WORK = 3
PAIRS = 16
UNITS = 12
RING = 4


class Batch:

    def __init__(self, o, it=None):
        self.o, self.it, self.par = o, it, o % 2

    def plus(self, k):
        return Batch(self.o + k, self.it)

    def index(self):
        return self.o if self.it is None else self.it * 2 + self.o

    def count(self, per, n):
        c = per * self.o + n
        if self.it is None:
            return max(c, 0)
        assert c >= 0
        return self.it * (2 * per) + c

    def pair_count(self, per):
        c = per * (self.o // 2)
        if self.it is None:
            return max(c, 0)
        assert c >= 0
        return self.it * per + c


def rows_of_slot(s, j):
    quad, halves = ((j // 3 + 1, (1, 2)), (j // 3 + 1, (3,)), (j // 3 + 2, (0,)))[j % 3]
    if quad < UNITS // 3:
        return [(s.batch, 4 * quad + i) for i in halves] if s.scan else []
    return [(s.batch.plus(1), 4 * (quad - UNITS // 3) + i) for i in halves] if s.ahead else []


class Step:

    def __init__(self, batch, first, ahead=True, scan=True, behind=True):
        self.batch, self.ahead, self.scan, self.behind = batch, ahead, scan, behind
        kinds = (AHEAD if ahead else {}) | (BEHIND if behind else {})
        self.items = {x: first + i for i, x in enumerate(x for x in ORDER if x[0] in kinds)}
        self.first, self.end = first, first + len(self.items)

    def work(self, item, it="own"):
        n = self.items[item] if isinstance(item, str) else self.first - item
        it = self.batch.it if isinstance(it, str) else it
        uses = n // WORK
        return n % WORK, uses if it is None else it * (2 * len(ORDER) // WORK) + uses


def wait(eng, sem, value):
    if not (isinstance(value, int) and value <= 0):
        eng.wait_ge(sem, value)


def build(nc, img_d, txt_d, convw_d, convb_d, pos_d, posid_d, emb_d, win_d, wx_d, wdt_d, bdt_d, alog_d, dskip_d,
          wout_d, gamma_d, beta_d, wfcT_d, bfc_d, wprojT_d, bproj_d, ae_d, ar_d, out_d):
    NB, _, KT, NPATCH = img_d.shape
    NTXT = txt_d.shape[1]
    NTOK, C = out_d.shape[1:]
    DI, NS = alog_d.shape
    R = wdt_d.shape[0]
    H = wfcT_d.shape[1]
    V = emb_d.shape[0]
    TP = NPATCH // 2
    TOK = [(0, TP), (TP, TP), (NPATCH, NTXT)]
    KD = DI // P
    KH = H // P
    CH = C // 2
    NQ = 4
    QS = NS // NQ
    IMGW = KT * NPATCH + P - TP + (NPATCH - 2 * TP)
    assert NTXT == P and KD == 3 and NQ * KD == UNITS and NQ * 4 == PAIRS and 2 * CH == C and NB % 2 == 0

    with ExitStack() as ctx:
        def sb(name, shape, dt=F32):
            return ctx.enter_context(nc.sbuf_tensor(name, shape, dt))

        def sem(name):
            return ctx.enter_context(nc.semaphore(name))

        y_ps = ctx.enter_context(nc.psum_tensor("y_ps", [P, KD, BANK], F32))
        row_ps = ctx.enter_context(nc.psum_tensor("row_ps", [P, 2, BANK], F32))
        work = [ctx.enter_context(nc.psum_tensor(f"work{i}", [P, BANK], F32)) for i in range(WORK)]

        ident = sb("ident", [P, P])
        row_sel = sb("row_sel", [96, 2 * NS, P], BF16)
        convw = sb("convw", [P, KT, C])
        pos = sb("pos", [P, 2, C])
        w_in = sb("w_in", [CH, 2, 2 * DI])
        w_dt_rows = sb("w_dt_rows", [P, KD, R])
        w_bc = sb("w_bc", [P, KD, 3, 2 * NS])
        w_dt = sb("w_dt", [R, DI])
        b_dt = sb("b_dt", [P, KD])
        d_skip = sb("d_skip", [P, KD])
        A = sb("A", [P, KD, NS])
        d_diag = sb("d_diag", [P, KD, P])
        w_out = sb("w_out", [P, KD, C])
        gamma = sb("gamma", [P, C])
        beta = sb("beta", [P, C])
        w0 = sb("w0", [CH, 2, H])
        b0 = sb("b0", [P, KH])
        w1 = sb("w1", [P, KH, C])
        b1 = sb("b1", [P, C])
        row_table = sb("row_table", [P, NB], I32)
        minus_half = sb("minus_half", [P, 3])
        small = sb("small", [P, 128])
        padded = sb("padded", [P, NTXT + 64], I32)

        img = sb("img", [P, 2, IMGW])
        h = sb("h", [P, 2, 3, C])
        xn = sb("xn", [P, 2, 3, C])
        h_post = sb("h_post", [P, 3, C])
        x_post = sb("x_post", [P, 3, C])
        res = sb("res", [P, 3, C])
        xn2 = sb("xn2", [P, 3, C])
        obuf = sb("obuf", [P, 2, 3, C])
        txt_row = sb("txt_row", [P, 1], I32)
        txt_tok = sb("txt_tok", [P, 1], I32)
        txt_emb = sb("txt_emb", [P, C])
        stats = sb("stats", [P, 3, 3, 6])
        mv = sb("mv", [P, 3, 3, 2])
        veps = sb("veps", [P, 3, 3])
        rstd = sb("rstd", [P, 3, 3])
        xT = sb("xT", [CH, 2, NTOK])
        x2T = sb("x2T", [CH, 2, NTOK])
        th = sb("th", [P, 2 * KD, NTOK])
        xz = sb("xz", [P, 2, 2 * KD, NTOK])
        dt_rows = sb("dt_rows", [R, NTOK])
        bc3 = sb("bc3", [96, 2, NTOK], BF16)
        bc_rest = sb("bc_rest", [96, NTOK])
        bc_mid = sb("bc_mid", [96, NTOK], BF16)
        relu = sb("relu", [P, KD, NTOK])
        corr = sb("corr", [P, KD, NTOK])
        dt = sb("dt", [P, 2, KD, NTOK])
        u = sb("u", [P, 2, KD, NTOK])
        rings = sb("rings", [P, 2, RING, QS * NTOK])
        dA = rings[:, 0, :, :].rearrange("p r (n t) -> p r n t", n=QS)
        w_bc3 = w_bc[:, :, :, :].rearrange("p k a n -> p k (a n)")
        st = rings[:, 1, :, :].rearrange("p r (n t) -> p r n t", n=QS)
        Bq = sb("Bq", [P, 2, QS, NTOK])
        Cq = sb("Cq", [P, 2, QS, NTOK])
        yz = sb("yz", [P, KD, NTOK])
        gT = sb("gT", [P, KH, NTOK])

        filled = [sem(f"filled{i}") for i in range(WORK)]
        drained = [sem(f"drained{i}") for i in range(WORK)]
        img_in = [sem(f"img_in{i}") for i in range(2)]
        out_stored = [sem(f"out_stored{i}") for i in range(2)]
        row_ready = sem("row_ready")
        tok_in = sem("tok_in")
        emb_in = sem("emb_in")
        txt_copied = sem("txt_copied")
        posted = sem("posted")
        stat_done = [sem(f"stat_done{i}") for i in range(3)]
        mv_done = [sem(f"mv_done{i}") for i in range(3)]
        veps_done = [sem(f"veps_done{i}") for i in range(3)]
        rstd_done = [sem(f"rstd_done{i}") for i in range(3)]
        xn_done = sem("xn_done")
        th_done = sem("th_done")
        bc_hi = sem("bc_hi")
        bc_left = sem("bc_left")
        bc_q = sem("bc_q")
        bc_lo = sem("bc_lo")
        abs_done = sem("abs_done")
        sp_act = sem("sp_act")
        sp_fix = sem("sp_fix")
        dt_done = sem("dt_done")
        u_done = sem("u_done")
        rows_mm = sem("rows_mm")
        rows_out = sem("rows_out")
        dA_done = sem("dA_done")
        dBx_done = sem("dBx_done")
        scan_done = sem("scan_done")
        prod_done = sem("prod_done")
        ysum_done = sem("ysum_done")
        y_read = sem("y_read")
        normed = sem("normed")
        scaled = sem("scaled")
        h2_done = sem("h2_done")
        xn2_done = sem("xn2_done")
        h2b_done = sem("h2b_done")
        weights_in = sem("weights_in")
        vectors_in = sem("vectors_in")
        txt_loaded = sem("txt_loaded")
        pos_in = sem("pos_in")
        top_in = sem("top_in")
        pool_prep = sem("pool_prep")
        dve_prep = sem("dve_prep")
        act_prep = sem("act_prep")
        pe_prep = sem("pe_prep")

        PRE = Step(Batch(-1), 0, scan=False, behind=False)
        FIRST = Step(Batch(0), PRE.end, behind=False)

        def odd(it):
            return Step(Batch(1, it), FIRST.end)

        def even(it):
            return Step(Batch(2, it), odd(it).end)

        LOOPS = NB // 2 - 1
        after = FIRST.end + LOOPS * 2 * len(ORDER)
        LAST = Step(Batch(NB - 1), after, ahead=False)
        POST = Step(Batch(NB), LAST.end, ahead=False, scan=False)
        assert FIRST.end % WORK == 0

        def run(eng, step):
            step(PRE)
            step(FIRST)
            with eng.Fori(0, LOOPS) as it:
                step(odd(it))
                step(even(it))
            step(LAST)
            step(POST)

        def wait_filled(eng, s, item):
            bank, uses = s.work(item)
            wait(eng, filled[bank], uses + 1)
            return work[bank]

        def wait_drained(eng, s, item):
            bank, uses = s.work(item)
            wait(eng, drained[bank], uses + 1)

        def wait_alone(eng, sem, value):
            if isinstance(value, int):
                wait(eng, sem, value)
            else:
                value = eng.to_reg(value)
                eng.wait_ge(dve_prep, ALL_DVE)
                eng.wait_ge(sem, value)

        def drains(s, item):
            return drained[s.work(item)[0]]

        E = 32
        NE = E * NTXT
        space = rings[:, :, :, :].rearrange("p a r x -> p (a r x)")
        match = space[:, 0:NE]
        place = space[:, NE:2 * NE].bitcast(I32)
        txt = obuf[:, 0, 0, 0:NTXT].bitcast(I32)
        best = xn2[:, :, 0:NTXT]
        best_i = h_post[:, 0, 0:NTXT].bitcast(I32)
        row_base = h_post[:, 1, 0:NTXT].bitcast(I32)
        rows_f = h_post[:, 2, 0:NTXT]
        none_f = x_post[:, 0, 0:NTXT]
        wx_raw = th[:, 0, 0:KD * (R + 2 * NS)].rearrange("p (k n) -> p k n", k=KD)
        pos_id = small[:, 0:2].bitcast(I32)
        alpha_e = small[:, 2:5]
        alpha_r = small[:, 5:8]
        coef = small[:, 8:17].rearrange("p (i j) -> p i j", i=3)
        half_mask = small[:, 17:18]
        ones = small[:, 18:19]
        g_cols = small[:, 20:20 + 3 * KH].rearrange("p (i m) -> p i m", i=3)
        c1 = small[:, 40:43]
        G = Bq[:, :, :, :].rearrange("p a n t -> p (a n t)")[:, 0:3 * H].rearrange("p (i h) -> p i h", i=3)
        convb = res[:, 0, :]

        block = ctx.enter_context(nc.Block())

        @block.sync
        def _(sp):
            sp.wait_ge(pool_prep, 1)
            for half in range(2):
                q = slice(64 * half, 64 * half + 64)
                sp.dma_start(txt[q, :], txt_d).then_inc(txt_loaded, 16)
                sp.dma_start(padded[q, 64 + 64 * half:64 + NTXT], txt_d[:, 0:NTXT - 64 * half]).then_inc(txt_loaded, 16)
            sp.wait_ge(dve_prep, 1)
            for b in range(2):
                sp.dma_start(img[:, b, 0:KT * NPATCH], img_d[b].rearrange("p k t -> p (k t)")).then_inc(img_in[b], 16)
            sp.dma_start(convw[:], convw_d).then_inc(weights_in, 16)
            sp.dma_start(w_in[:], win_d.rearrange("(k p) n -> p k n", k=2)).then_inc(weights_in, 16)
            sp.dma_start(wx_raw, wx_d.rearrange("(k p) n -> p k n", p=P)).then_inc(weights_in, 16)
            sp.dma_start(w_dt[:], wdt_d).then_inc(weights_in, 16)
            sp.dma_start(w_out[:], wout_d.rearrange("(k p) n -> p k n", p=P)).then_inc(weights_in, 16)
            sp.dma_start(w0[:], wfcT_d.rearrange("(k p) n -> p k n", k=2)).then_inc(weights_in, 16)
            sp.dma_start(w1[:], wprojT_d.rearrange("(k p) n -> p k n", p=P)).then_inc(weights_in, 16)
            sp.dma_start(A[:], alog_d.rearrange("(k p) n -> p k n", p=P)).then_inc(weights_in, 16)
            sp.wait_ge(dve_prep, TOPS)
            sp.dma_start(best[0:64, 1, :], best[64:128, 0, :]).then_inc(top_in, 16)

            def load(c, s, it):
                bank, uses = s.work("P1", it)
                wait(sp, filled[bank], uses + 1)
                sp.dma_start(img[:, c.par, 0:KT * NPATCH], img_d[c.index()].rearrange("p k t -> p (k t)"))\
                  .then_inc(img_in[c.par], 16)

            def store(c, s, it):
                for g in range(2):
                    bank, uses = s.work(f"G{g}", it)
                    wait(sp, drained[bank], uses + 1)
                sp.dma_start(out_d[c.index(), 0:NPATCH, :].rearrange("(t p) c -> p t c", p=TP),
                             obuf[0:TP, c.par, 0:2, :]).then_inc(out_stored[c.par], 16)
                sp.dma_start(out_d[c.index(), NPATCH:NTOK, :], obuf[:, c.par, 2, :])\
                  .then_inc(out_stored[c.par], 16)

            load(Batch(2), PRE, None)
            load(Batch(3), FIRST, None)
            with sp.Fori(0, NB // 2 - 2) as it:
                for o in range(2):
                    s = (odd, even)[o](it)
                    store(Batch(o, it), s, it)
                    wait_alone(sp, out_stored[o], it * 32 + 32)
                    load(Batch(4 + o, it), s, it)
            for b in range(NB - 4, NB - 2):
                it = b // 2
                s = (odd, even)[b % 2](0)
                store(Batch(b), s, it)
            store(Batch(NB - 2), LAST, None)
            store(Batch(NB - 1), POST, None)
            for q in range(2):
                sp.wait_ge(out_stored[q], 32 * (NB // 2))

        @block.gpsimd
        def _(pool):
            prep = [0]

            def link(ins):
                ins.then_inc(pool_prep, 1)
                prep[0] += 1
                pool.wait_ge(pool_prep, prep[0])

            link(nc.gpsimd.memset(padded[:], -1))
            pool.dma_start(pos_id[0:TP, :], posid_d).then_inc(pos_in, 16)
            for dst, src in ((alpha_e, ae_d), (alpha_r, ar_d), (gamma[:], gamma_d), (beta[:], beta_d),
                             (b1[:], bproj_d), (convb, convb_d)):
                pool.dma_start(dst, src.partition_broadcast(P)).then_inc(vectors_in, 16)
            for dst, src in ((b_dt, bdt_d), (d_skip, dskip_d), (b0, bfc_d)):
                pool.dma_start(dst[:], src).then_inc(vectors_in, 16)
            link(nc.gpsimd.iota(place[0:64, :], pattern=[[1, E], [1, NTXT]], base=-64, channel_multiplier=0))
            link(nc.gpsimd.iota(place[64:128, :], pattern=[[1, E], [1, NTXT]], base=-128, channel_multiplier=0))
            link(nc.gpsimd.iota(row_base[0:64, :], pattern=[[0, NTXT]], base=1, channel_multiplier=NTXT))
            link(nc.gpsimd.memset(ident[:], 0.0))
            link(nc.gpsimd.affine_select(out=ident[:], in_=ident[:], compare_op=ALU.not_equal, fill=1.0, base=0,
                                         pattern=[[-1, P]], channel_multiplier=1))
            link(nc.gpsimd.memset(row_sel[:], 0.0))
            for part in range(3):
                link(nc.gpsimd.affine_select(out=row_sel[:], in_=row_sel[:], compare_op=ALU.not_equal, fill=1.0,
                                             base=-2 * NS * part, pattern=[[-1, 2 * NS], [0, P]],
                                             channel_multiplier=1))
            link(nc.gpsimd.memset(ones, 1.0))
            link(nc.gpsimd.memset(half_mask, 1.0))
            link(nc.gpsimd.affine_select(out=half_mask, in_=half_mask, compare_op=ALU.is_ge, fill=0.0,
                                         base=EMBED_CHOICES[1] - CH - 1, pattern=[[0, 1]], channel_multiplier=-1))
            link(nc.gpsimd.memset(minus_half[:], -0.5))
            link(nc.gpsimd.memset(pos[:], 0.0))
            assert prep[0] == POOL_CONST
            pool.wait_ge(pos_in, 16)
            for t in range(2):
                pool.indirect_dma_start(pos[0:TP, t, :], None, pos_d, bass.IndirectOffsetOnAxis(
                    ap=pos_id[0:TP, t:t + 1], axis=0)).then_inc(pos_in, 16)
            pool.wait_ge(dve_prep, CHUNK0)
            link(nc.gpsimd.iota(place[0:64, :], pattern=[[1, E], [1, NTXT]], base=E - 64, channel_multiplier=0))
            link(nc.gpsimd.iota(place[64:128, :], pattern=[[1, E], [1, NTXT]], base=E - 128, channel_multiplier=0))
            pool.wait_ge(dve_prep, ALL_DVE)

            def norm(b, which):
                wait_alone(pool, mv_done[which], b.count(3, 3))
                nc.gpsimd.tensor_scalar(veps[:, which, :], mv[:, which, :, 1], EPS, None, ALU.add)\
                    .then_inc(veps_done[which], 1)
                pool.wait_ge(veps_done[which], b.count(1, 1))
                nc.gpsimd.tensor_tensor(rstd[:, which, :], veps[:, which, :], minus_half[:], ALU.pow)\
                    .then_inc(rstd_done[which], 1)

            def step(s):
                a, c = s.batch.plus(1), s.batch.plus(-1)
                for j in range(UNITS):
                    if j == 0 and s.ahead:
                        wait_alone(pool, txt_copied, a.count(1, 0))
                        nc.gpsimd.tensor_copy(txt_row[:], row_table[:, bass.ds(a.index(), 1)]).then_inc(row_ready, 1)
                        nc.gpsimd.memset(txt_tok[:], NO_ROW).then_inc(row_ready, 1)
                        nc.gpsimd.memset(txt_emb[:], 0.0).then_inc(row_ready, 1)
                        wait_alone(pool, row_ready, a.count(3, 3))
                        pool.indirect_dma_start(txt_tok[:], None, txt_d.rearrange("b (t o) -> (b t) o", o=1),
                                                bass.IndirectOffsetOnAxis(ap=txt_row[:, 0:1], axis=0),
                                                bounds_check=NB * NTXT - 1, oob_is_err=False).then_inc(tok_in, 16)
                    if j == 0 and s.behind:
                        wait_drained(pool, s, 2)
                        wait_drained(pool, s, 1)
                        wait(pool, xn_done, c.count(3, 3))
                        nc.gpsimd.tensor_tensor(h_post[:], h[:, c.par], beta[:, None, :].broadcast_to([P, 3, C]),
                                                ALU.add).then_inc(posted, 1)
                        nc.gpsimd.tensor_copy(x_post[:], xn[:, c.par]).then_inc(posted, 1)
                    if j == 0 and s.ahead:
                        wait_alone(pool, tok_in, a.count(16, 16))
                        pool.indirect_dma_start(txt_emb[:], None, emb_d,
                                                bass.IndirectOffsetOnAxis(ap=txt_tok[:, 0:1], axis=0),
                                                bounds_check=V - 1, oob_is_err=False).then_inc(emb_in, 16)
                        pool.wait_ge(emb_in, a.count(16, 16))
                        wait_alone(pool, posted, a.plus(-2).count(2, 2))
                        nc.gpsimd.tensor_copy(h[:, a.par, 2, :], txt_emb[:]).then_inc(txt_copied, 1)
                    if j == 1 and s.ahead:
                        norm(a, 0)
                    if j == 3 and s.behind:
                        norm(c, 1)
                        norm(c, 2)
                        pool.wait_ge(h2_done, c.count(1, 1))
                        nc.gpsimd.tensor_tensor(h_post[:], res[:], b1[:, None, :].broadcast_to([P, 3, C]),
                                                ALU.add).then_inc(h2b_done, 1)
                    if j == 6 and s.ahead:
                        if s.behind:
                            wait_alone(pool, h2b_done, c.count(1, 1))
                        wait_alone(pool, bc_left, a.count(1, 1))
                        nc.gpsimd.tensor_copy(bc3[32:64, a.par], bc_rest[32:64, :]).then_inc(bc_lo, 1)
                        nc.gpsimd.tensor_copy(bc_mid[64:96, :], bc_rest[64:96, :]).then_inc(bc_q, 1)
                        pool.wait_ge(bc_q, a.count(1, 1))
                        nc.gpsimd.tensor_tensor(bc3[64:96, a.par], bc_rest[64:96, :], bc_mid[64:96, :],
                                                ALU.subtract).then_inc(bc_lo, 1)
                        pool.wait_ge(bc_lo, a.count(2, 2))

            run(pool, step)

        @block.scalar
        def _(act):
            act.wait_ge(weights_in, WEIGHTS)
            act.wait_ge(vectors_in, VECTORS)
            nc.scalar.activation(A[:], A[:], ACT.Exp).then_inc(act_prep, 1)
            act.wait_ge(act_prep, 1)
            nc.scalar.activation(A[:], A[:], ACT.Copy, scale=-1.0).then_inc(act_prep, 1)
            nc.scalar.activation(w_dt_rows[:], wx_raw[:, :, 0:R], ACT.Copy, scale=0.5).then_inc(act_prep, 1)
            for part in range(3):
                nc.scalar.activation(w_bc[:, :, part, :], wx_raw[:, :, R:R + 2 * NS], ACT.Copy, scale=0.5)\
                    .then_inc(act_prep, 1)
            nc.scalar.activation(w_out[:], w_out[:], ACT.Copy, scale=0.5).then_inc(act_prep, 1)
            act.wait_ge(act_prep, 7)
            act.wait_ge(dve_prep, ALL_DVE)
            nc.scalar.preload_act_table_set("exp_and_others")

            def decay(b, j):
                q, k, r = j // KD, j % KD, j % RING
                if j == 0:
                    act.wait_ge(dt_done, b.count(1, 1))
                wait(act, scan_done, b.count(UNITS, j + 1 - RING))
                for i in range(QS):
                    n = q * QS + i
                    last = nc.scalar.activation(dA[:, r, i, 1:NTOK], dt[:, b.par, k, 1:NTOK], ACT.Exp,
                                                scale=A[:, k, n:n + 1])
                last.then_inc(dA_done, 1)

            def rows(b, pair):
                q, kind, half = pair // 4, pair % 4 // 2, pair % 2
                act.wait_ge(rows_mm, b.count(PAIRS, pair + 1))
                wait(act, (dBx_done, prod_done)[kind], b.count(UNITS, KD * (q - 1)))
                dst = (Bq, Cq)[kind]
                nc.scalar.activation(dst[:, q % 2, 2 * half:2 * half + 2, :], row_ps[:, :, 0:NTOK], ACT.Copy)\
                    .then_inc(rows_out, 1)

            def step(s):
                a, c = s.batch.plus(1), s.batch.plus(-1)

                def tanh(names):
                    for m in names:
                        bank = wait_filled(act, s, f"M{m}")
                        nc.scalar.activation(th[:, m, :], bank[:, 0:NTOK], ACT.Tanh, scale=0.5).then_inc(th_done, 1)

                def gelu(names):
                    for m in names:
                        bank = wait_filled(act, s, f"F{m}")
                        nc.scalar.activation(gT[:, m, :], bank[:, 0:NTOK], ACT.Gelu_apprx_tanh, bias=b0[:, m:m + 1])\
                            .then_inc(drains(s, f"F{m}"), 1)

                def decay_of(n):
                    if n < UNITS:
                        if s.scan:
                            decay(s.batch, n)
                    elif s.ahead:
                        decay(a, n - UNITS)

                for j in range(UNITS):
                    if j in (0, 10, 11):
                        decay_of(j + 2)
                    pairs = rows_of_slot(s, j)
                    if j == 9:
                        for i in range(2):
                            for b, pair in pairs[i:i + 1]:
                                rows(b, pair)
                            decay_of(10 + i)
                    elif j != 6:
                        for b, pair in pairs:
                            rows(b, pair)
                    if j == 7:
                        decay_of(9)
                    if j == 7 and s.behind:
                        nc.scalar.preload_act_table_set("gelu_apprx_tanh_and_others")
                        gelu(range(0, KH // 2))
                    if j == 8:
                        if s.behind:
                            gelu(range(KH // 2, KH))
                        if s.ahead:
                            nc.scalar.preload_act_table_set("natural_log")
                            act.wait_ge(sp_act, a.count(3, 2))
                            nc.scalar.activation(dt[:, a.par], th[:, KD:2 * KD], ACT.Ln).then_inc(sp_act, 1)
                        nc.scalar.preload_act_table_set("exp_and_others")
                    if 1 <= j <= 5:
                        decay_of(j + 2)
                    if j == 2 and s.ahead:
                        for k in range(2):
                            bank = wait_filled(act, s, f"T{k}")
                            nc.scalar.activation(xT[:, k, :], bank[0:CH, 0:NTOK], ACT.Copy)\
                                .then_inc(drains(s, f"T{k}"), 1)
                    if j == 3 and s.ahead:
                        wait(act, sp_fix, a.count(2, 0))
                        tanh(range(0, 3))
                    if j == 4 and s.ahead:
                        tanh(range(3, 6))
                    if j == 5 and s.ahead:
                        bank = wait_filled(act, s, "X0")
                        nc.scalar.activation(dt_rows[:], bank[0:R, 0:NTOK], ACT.Copy).then_inc(drains(s, "X0"), 1)
                        bank = wait_filled(act, s, "X1")
                        nc.scalar.activation(bc3[:, a.par], bank[0:96, 0:NTOK], ACT.Copy).then_inc(bc_hi, 1)
                        wait(act, bc_lo, a.count(2, 0))
                        nc.scalar.activation(bc_rest[:], bank[0:96, 0:NTOK], ACT.Copy).then_inc(drains(s, "X1"), 1)
                    if j == 6:
                        for b, pair in pairs[0:1]:
                            rows(b, pair)
                        if s.behind:
                            for k in range(2):
                                bank = wait_filled(act, s, f"U{k}")
                                nc.scalar.activation(x2T[:, k, :], bank[0:CH, 0:NTOK], ACT.Copy)\
                                    .then_inc(drains(s, f"U{k}"), 1)
                        decay_of(8)
                        for b, pair in pairs[1:2]:
                            rows(b, pair)
                    if j == 6 and s.ahead:
                        for k in range(KD):
                            bank = wait_filled(act, s, f"D{k}")
                            nc.scalar.activation(th[:, k, :], bank[:, 0:NTOK], ACT.Abs, bias=b_dt[:, k:k + 1])\
                                .then_inc(abs_done, 1)
                            nc.scalar.activation(relu[:, k, :], bank[:, 0:NTOK], ACT.Relu, bias=b_dt[:, k:k + 1])\
                                .then_inc(drains(s, f"D{k}"), 1)
                        act.wait_ge(abs_done, a.count(3, 3))
                        nc.scalar.activation(th[:, 0:KD], th[:, 0:KD], ACT.Exp, scale=-1.0).then_inc(sp_act, 1)
                        act.wait_ge(sp_act, a.count(3, 1))
                        wait_drained(act, s, f"M{2 * KD - 1}")
                        nc.scalar.activation(th[:, KD:2 * KD], th[:, 0:KD], ACT.Identity, bias=1.0)\
                            .then_inc(sp_act, 1)

            run(act, step)

        @block.tensor
        def _(pe):
            pe.wait_ge(dve_prep, G_READY)
            pe.wait_ge(pool_prep, POOL_CONST)
            for i in range(3):
                for m in range(KH):
                    last = nc.tensor.matmul(work[0][:, i * KH + m:i * KH + m + 1], G[0:1, i, m * P:(m + 1) * P],
                                            ones[0:1, :], start=True, stop=True)
            last.then_inc(pe_prep, 1)
            pe.wait_ge(dve_prep, ROWS_READY)
            nc.tensor.transpose(work[1][:, 0:64], rows_f[0:64, :], ident[0:64, 0:64]).then_inc(pe_prep, 1)
            pe.wait_ge(act_prep, 7)
            pe.wait_ge(dve_prep, ALL_DVE)

            def begin(s, item):
                bank, uses = s.work(item)
                wait(pe, drained[bank], uses)
                return work[bank], filled[bank]

            def ysum(b, j):
                q, k, r = j // KD, j % KD, j % RING
                pe.wait_ge(prod_done, b.count(UNITS, j + 1))
                if q == 0:
                    wait(pe, y_read, b.count(KD, k + 1 - KD))
                    nc.tensor.matmul(y_ps[:, k, 0:NTOK], d_diag[:, k, :], xz[:, b.par, k, :], start=True, stop=False)
                for i in range(QS):
                    last = nc.tensor.matmul(y_ps[:, k, 0:NTOK], ident[:], st[:, r, i, :],
                                            start=False, stop=(q == NQ - 1 and i == QS - 1))
                last.then_inc(ysum_done, 1)

            def rows(b, pair):
                q, kind, half = pair // 4, pair % 4 // 2, pair % 2
                if pair == 0:
                    pe.wait_ge(bc_hi, b.count(1, 1))
                    pe.wait_ge(bc_lo, b.count(2, 2))
                wait(pe, rows_out, b.count(PAIRS, pair))
                for i in range(2):
                    n = kind * NS + q * QS + 2 * half + i
                    last = nc.tensor.matmul(row_ps[:, i, 0:NTOK], row_sel[:, n, :], bc3[:, b.par, :],
                                            start=True, stop=True)
                last.then_inc(rows_mm, 1)

            def step(s):
                a, c = s.batch.plus(1), s.batch.plus(-1)

                def project(names, weights, x, width):
                    for m in names:
                        bank, full = begin(s, f"{width}{m}")
                        for k in range(2):
                            last = nc.tensor.matmul(bank[:, 0:NTOK], weights[:, k, m * P:(m + 1) * P], x[:, k, :],
                                                    start=(k == 0), stop=(k == 1))
                        last.then_inc(full, 1)

                def turn(item, x):
                    for k in range(2):
                        bank, full = begin(s, f"{item}{k}")
                        for t, (t0, n) in enumerate(TOK):
                            last = nc.tensor.transpose(bank[0:CH, t0:t0 + n], x[0:n, t, k * CH:(k + 1) * CH],
                                                       ident[0:n, 0:n])
                        last.then_inc(full, 1)

                def to_tokens(item, x, weights, n, banks=(0, 1)):
                    for g in banks:
                        tiles = ((0, 1), (2,))[g]
                        bank, full = begin(s, f"{item}{g}")
                        for i, t in enumerate(tiles):
                            t0 = TOK[t][0]
                            for k in range(n):
                                last = nc.tensor.matmul(bank[:, i * C:(i + 1) * C], x[:, k, t0:t0 + P],
                                                        weights[:, k, :], start=(k == 0), stop=(k == n - 1))
                        last.then_inc(full, 1)

                for j in range(UNITS):
                    if j == 0 and s.behind:
                        ysum(c, UNITS - 1)
                    if j == 0 and s.ahead:
                        pe.wait_ge(img_in[a.par], a.plus(2).pair_count(16))
                        for t in range(2):
                            bank, full = begin(s, f"P{t}")
                            for k in range(KT):
                                t0 = k * NPATCH + t * TP
                                last = nc.tensor.matmul(bank[:, 0:C], img[:, a.par, t0:t0 + P], convw[:, k, :],
                                                        start=(k == 0), stop=(k == KT - 1))
                            last.then_inc(full, 1)
                    if j == 6 and s.behind:
                        pe.wait_ge(xn2_done, c.count(3, 3))
                        turn("U", xn2)
                    if j == 10 and s.behind:
                        to_tokens("G", gT, w1, KH, (1,))
                    pairs = rows_of_slot(s, j)
                    if pairs:
                        rows(*pairs[0])
                    if s.scan and j >= 1:
                        ysum(s.batch, j - 1)
                    if len(pairs) > 1:
                        rows(*pairs[1])
                    if j == 2 and s.ahead:
                        pe.wait_ge(xn_done, a.count(3, 3))
                        turn("T", xn[:, a.par])
                    if j == 2 and s.behind:
                        pe.wait_ge(y_read, c.count(KD, KD))
                        to_tokens("O", yz, w_out, KD)
                    if j == 3 and s.ahead:
                        wait_drained(pe, s, "T1")
                        project(range(0, 3), w_in, xT, "M")
                    if j == 4 and s.ahead:
                        project(range(3, 6), w_in, xT, "M")
                    if j == 5 and s.ahead:
                        wait_drained(pe, s, "M2")
                        for item, rows_of, n in (("X0", w_dt_rows, R), ("X1", w_bc3, 96)):
                            bank, full = begin(s, item)
                            for k in range(KD):
                                last = nc.tensor.matmul(bank[0:n, 0:NTOK], rows_of[:, k, :], xz[:, a.par, k, :],
                                                        start=(k == 0), stop=(k == KD - 1))
                            last.then_inc(full, 1)
                    if j == 6 and s.ahead:
                        wait_drained(pe, s, "X0")
                        for k in range(KD):
                            bank, full = begin(s, f"D{k}")
                            nc.tensor.matmul(bank[:, 0:NTOK], w_dt[:, k * P:(k + 1) * P], dt_rows[:],
                                             start=True, stop=True).then_inc(full, 1)
                    if j == 7 and s.behind:
                        wait_drained(pe, s, "U1")
                        project(range(0, KH // 2), w0, x2T, "F")
                    if j == 8 and s.behind:
                        project(range(KH // 2, KH), w0, x2T, "F")
                    if j == 9 and s.behind:
                        wait_drained(pe, s, "F5")
                        to_tokens("G", gT, w1, KH, (0,))

            run(pe, step)

        @block.vector
        def _(dve):
            prep = [0]

            def link(ins):
                ins.then_inc(dve_prep, 1)
                prep[0] += 1
                dve.wait_ge(dve_prep, prep[0])

            link(nc.vector.memset(img[:], 0.0))
            dve.wait_ge(weights_in, WEIGHTS)
            dve.wait_ge(vectors_in, VECTORS)
            dve.wait_ge(pool_prep, POOL_CONST)
            for i in range(3):
                link(nc.vector.tensor_scalar(coef[:, i, :], alpha_r, alpha_e[:, i:i + 1], None, ALU.mult))
            link(nc.vector.memset(G, 0.0))
            for i, e in enumerate(EMBED_CHOICES):
                for j, r in enumerate(RATIO_CHOICES):
                    link(nc.vector.tensor_scalar(G[:, i, 0:r * e], G[:, i, 0:r * e], coef[:, i, j:j + 1], None,
                                                 ALU.add))
            assert prep[0] == G_READY
            scr = gT[:, :, :].rearrange("p m t -> p (m t)")[:, 0:H]
            link(nc.vector.scalar_tensor_tensor(scr[0:CH, :], G[0:CH, 1, :], half_mask[0:CH, :], G[0:CH, 2, :],
                                                ALU.mult, ALU.add))
            link(nc.vector.tensor_tensor(w0[:, 1, :], w0[:, 1, :], scr[0:CH, :], ALU.mult))
            link(nc.vector.tensor_tensor(scr[0:CH, :], G[0:CH, 0, :], G[0:CH, 1, :], ALU.add))
            link(nc.vector.tensor_tensor(scr[0:CH, :], scr[0:CH, :], G[0:CH, 2, :], ALU.add))
            link(nc.vector.tensor_tensor(w0[:, 0, :], w0[:, 0, :], scr[0:CH, :], ALU.mult))
            dve.wait_ge(pe_prep, 1)
            link(nc.vector.tensor_copy(g_cols, work[0][:, 0:3 * KH].rearrange("p (i m) -> p i m", i=3)))
            for i in (1, 0):
                link(nc.vector.tensor_tensor(g_cols[:, i, :], g_cols[:, i, :], g_cols[:, i + 1, :], ALU.add))
            link(nc.vector.tensor_tensor(b0[:], b0[:], g_cols[:, 0, :], ALU.mult))
            link(nc.vector.tensor_reduce(c1, coef, AX.X, ALU.add))
            for i in (1, 0):
                link(nc.vector.tensor_tensor(c1[:, i:i + 1], c1[:, i:i + 1], c1[:, i + 1:i + 2], ALU.add))
            lo = 0
            for i, e in enumerate(EMBED_CHOICES):
                link(nc.vector.tensor_tensor(w1[:, :, lo:e], w1[:, :, lo:e],
                                             g_cols[:, i, :, None].broadcast_to([P, KH, e - lo]), ALU.mult))
                link(nc.vector.tensor_scalar(b1[:, lo:e], b1[:, lo:e], c1[:, i:i + 1], None, ALU.mult))
                lo = e
            for k in range(KD):
                link(nc.vector.tensor_scalar(d_diag[:, k, :], ident[:], d_skip[:, k:k + 1], 0.5, ALU.mult, ALU.mult))
            dve.wait_ge(pos_in, 48)
            link(nc.vector.tensor_tensor(pos[:], pos[:], convb[:, None, :].broadcast_to([P, 2, C]), ALU.add))

            dve.wait_ge(txt_loaded, 64)
            for chunk in range(2):
                shifted = padded[:, chunk * E:chunk * E + NTXT]
                shifted = bass.AP(tensor=shifted.tensor, offset=shifted.offset,
                                  ap=[shifted.ap[0], [1, E], [1, NTXT]])
                m3 = match.rearrange("p (e i) -> p e i", e=E)
                link(nc.vector.tensor_tensor(m3, txt[:, None, :].broadcast_to([P, E, NTXT]), shifted, ALU.is_equal))
                link(nc.vector.tensor_tensor_scan(match, match, match, 0.0, ALU.mult, ALU.add))
                if chunk == 1:
                    dve.wait_ge(pool_prep, POOL_CONST + 2)
                link(nc.vector.scalar_tensor_tensor(match, match, float(NTXT), place, ALU.mult, ALU.add))
                link(nc.vector.tensor_reduce(best[:, chunk, :], match.rearrange("p (e i) -> p i e", e=E), AX.X,
                                             ALU.max))
                if chunk == 0:
                    assert prep[0] == CHUNK0
            link(nc.vector.tensor_tensor(best[:, 0, :], best[:, 0, :], best[:, 1, :], ALU.max))
            assert prep[0] == TOPS
            dve.wait_ge(top_in, 16)
            low = slice(0, 64)
            link(nc.vector.tensor_tensor(best[low, 0, :], best[low, 0, :], best[low, 1, :], ALU.max))
            link(nc.vector.tensor_copy(best_i[low, :], best[low, 0, :]))
            link(nc.vector.tensor_scalar(best_i[low, :], best_i[low, :], NTXT - 1, None, ALU.bitwise_and))
            link(nc.vector.tensor_tensor(rows_f[low, :], best_i[low, :], row_base[low, :], ALU.add))
            link(nc.vector.tensor_scalar(none_f[low, :], best[low, 0, :], float(NTXT), float(NO_ROW), ALU.is_lt,
                                         ALU.mult))
            link(nc.vector.tensor_tensor(rows_f[low, :], rows_f[low, :], none_f[low, :], ALU.add))
            assert prep[0] == ROWS_READY
            dve.wait_ge(pe_prep, 2)
            link(nc.vector.tensor_copy(row_table[:], work[1][:, 0:64]))
            link(nc.vector.memset(dA[:, :, :, 0:1], 0.0))
            assert prep[0] == ALL_DVE

            def normalise(b, which, x, out, done):
                dve.wait_ge(rstd_done[which], b.count(1, 1))
                for t in range(3):
                    nc.vector.tensor_scalar(out[:, t, :], x[:, t, :], mv[:, which, t, 0:1],
                                            rstd[:, which, t:t + 1], ALU.subtract, ALU.mult).then_inc(done, 1)

            def moments(b, which, x, last=None):
                for t in range(3):
                    if t == 2 and last is not None:
                        dve.wait_ge(*last)
                    nc.vector.bn_stats(stats[:, which, t, :], x[:, t, :]).then_inc(stat_done[which], 1)
                wait_alone(dve, stat_done[which], b.count(3, 3))
                for t in range(3):
                    nc.vector.bn_aggr(mv[:, which, t, :], stats[:, which, t, :]).then_inc(mv_done[which], 1)

            def drive(b, j):
                q, k, r = j // KD, j % KD, j % RING
                if j == 0:
                    dve.wait_ge(u_done, b.count(1, 1))
                if k == 0:
                    dve.wait_ge(rows_out, b.count(PAIRS, 4 * q + 2))
                wait(dve, ysum_done, b.count(UNITS, j + 1 - RING))
                nc.vector.tensor_tensor(st[:, r], u[:, b.par, k, None, :].broadcast_to([P, QS, NTOK]), Bq[:, q % 2],
                                        ALU.mult).then_inc(dBx_done, 1)

            def scan(b, j):
                r = j % RING
                dve.wait_ge(dA_done, b.count(UNITS, j + 1))
                dve.wait_ge(dBx_done, b.count(UNITS, j + 1))
                nc.vector.tensor_tensor_scan(rings[:, 1, r, :], rings[:, 0, r, :], rings[:, 1, r, :], 0.0,
                                             ALU.mult, ALU.add).then_inc(scan_done, 1)

            def weigh(b, j):
                q, r = j // KD, j % RING
                if j % KD == 0:
                    dve.wait_ge(rows_out, b.count(PAIRS, 4 * q + 4))
                dve.wait_ge(scan_done, b.count(UNITS, j + 1))
                nc.vector.tensor_tensor(st[:, r], st[:, r], Cq[:, q % 2], ALU.mult).then_inc(prod_done, 1)

            def step(s):
                a, c = s.batch.plus(1), s.batch.plus(-1)

                def gate(names):
                    for m in names:
                        bank = wait_filled(dve, s, f"M{m}")
                        dve.wait_ge(th_done, a.count(6, m + 1))
                        nc.vector.scalar_tensor_tensor(xz[:, a.par, m, :], th[:, m, :], 1.0, bank[:, 0:NTOK],
                                                       ALU.add, ALU.mult).then_inc(drains(s, f"M{m}"), 1)

                def gated_sums():
                    for k in range(KD):
                        dve.wait_ge(ysum_done, c.count(UNITS, UNITS - KD + k + 1))
                        nc.vector.tensor_tensor(yz[:, k, :], y_ps[:, k, 0:NTOK], xz[:, c.par, KD + k, :], ALU.mult)\
                            .then_inc(y_read, 1)

                def embed():
                    wait(dve, posted, a.plus(-2).count(2, 2))
                    for t in range(2):
                        bank = wait_filled(dve, s, f"P{t}")
                        nc.vector.tensor_tensor(h[:, a.par, t, :], bank[:, 0:C], pos[:, t, :], ALU.add)\
                            .then_inc(drains(s, f"P{t}"), 1)
                    wait_drained(dve, s, "P0")
                    wait_drained(dve, s, "P1")
                    moments(a, 0, h[:, a.par], (txt_copied, a.count(1, 1)))

                def sum_tokens(item, x, out):
                    for g, (t0, t1) in enumerate(((0, 2), (2, 3))):
                        bank = wait_filled(dve, s, f"{item}{g}")
                        nc.vector.tensor_tensor(out[:, t0:t1, :],
                                                bank[:, 0:(t1 - t0) * C].rearrange("p (t c) -> p t c", c=C),
                                                x[:, t0:t1, :], ALU.add).then_inc(drains(s, f"{item}{g}"), 1)

                def mixed():
                    dve.wait_ge(posted, c.count(2, 2))
                    sum_tokens("O", x_post, res)
                    wait_drained(dve, s, "O0")
                    wait_drained(dve, s, "O1")
                    moments(c, 1, res)

                def second():
                    normalise(c, 1, res, res, normed)
                    dve.wait_ge(normed, c.count(3, 3))
                    nc.vector.tensor_tensor(res[:], res[:], gamma[:, None, :].broadcast_to([P, 3, C]), ALU.mult)\
                        .then_inc(scaled, 1)
                    dve.wait_ge(scaled, c.count(1, 1))
                    nc.vector.tensor_tensor(res[:], res[:], h_post[:], ALU.add).then_inc(h2_done, 1)
                    dve.wait_ge(h2_done, c.count(1, 1))
                    moments(c, 2, res)

                def rest_of_rows():
                    dve.wait_ge(bc_hi, a.count(1, 1))
                    wait_drained(dve, s, "X1")
                    nc.vector.tensor_tensor(bc_rest[:], bc_rest[:], bc3[:, a.par], ALU.subtract)\
                        .then_inc(bc_left, 1)

                def rounding():
                    dve.wait_ge(sp_act, a.count(3, 2))
                    nc.vector.scalar_tensor_tensor(corr[:], th[:, KD:2 * KD], 1.0, th[:, 0:KD], ALU.subtract,
                                                   ALU.subtract).then_inc(sp_fix, 1)
                    dve.wait_ge(sp_fix, a.count(2, 1))
                    nc.vector.tensor_tensor(corr[:], relu[:], corr[:], ALU.subtract).then_inc(sp_fix, 1)

                def steps_of_time():
                    dve.wait_ge(sp_act, a.count(3, 3))
                    dve.wait_ge(sp_fix, a.count(2, 2))
                    nc.vector.tensor_tensor(dt[:, a.par], dt[:, a.par], corr[:], ALU.add).then_inc(dt_done, 1)
                    dve.wait_ge(dt_done, a.count(1, 1))
                    nc.vector.scalar_tensor_tensor(u[:, a.par], xz[:, a.par, 0:KD], 0.5, dt[:, a.par], ALU.mult,
                                                   ALU.mult).then_inc(u_done, 1)

                def output():
                    if c.it is None:
                        wait(dve, out_stored[c.par], c.pair_count(32))
                    dve.wait_ge(h2b_done, c.count(1, 1))
                    sum_tokens("G", h_post, obuf[:, c.par])

                for j in range(UNITS):
                    if j == 5 and s.ahead:
                        gate(range(3, 6))
                    if s.scan:
                        scan(s.batch, j)
                    if j == 1 and s.behind:
                        gated_sums()
                    if j == 2 and s.ahead:
                        dve.wait_ge(mv_done[0], a.count(3, 3))
                        normalise(a, 0, h[:, a.par], xn[:, a.par], xn_done)
                    if j == 3 and s.behind:
                        mixed()
                    if j == 4 and s.ahead:
                        gate(range(0, 3))
                    if j == 4 and s.behind:
                        second()
                    if j == 5 and s.behind:
                        normalise(c, 2, res, xn2, xn2_done)
                    if s.scan and j + 1 < UNITS:
                        drive(s.batch, j + 1)
                    if s.ahead and j + 1 == UNITS:
                        drive(a, 0)
                    if j == 1 and s.ahead:
                        embed()
                    if j == 7 and s.ahead:
                        rest_of_rows()
                    if j == 8 and s.ahead:
                        rounding()
                    if s.scan:
                        weigh(s.batch, j)
                    if j == 9 and s.ahead:
                        steps_of_time()
                    if j == 11 and s.behind:
                        output()

            run(dve, step)


WEIGHTS = 16 * 8
VECTORS = 16 * (6 + 3)
POOL_CONST = 15
G_READY = 1 + 3 + 1 + 9
CHUNK0 = G_READY + 5 + 1 + 2 + 1 + 1 + 2 + 6 + 3 + 1 + 4
TOPS = CHUNK0 + 4 + 1
ROWS_READY = TOPS + 6
ALL_DVE = ROWS_READY + 2


def kernel(x, x_txt, L0_tok_conv_w, L0_tok_conv_b, L0_tok_pos_table, L0_txt_emb, L0_attn_W_in, L0_attn_W_x,
           L0_attn_W_dt, L0_attn_b_dt, L0_attn_A_log, L0_attn_D_skip, L0_attn_W_out, L0_attn_gamma, L0_attn_beta,
           L0_ffn_w_fc, L0_ffn_b_fc, L0_ffn_w_proj, L0_ffn_b_proj, L0_ffn_alpha_e, L0_ffn_alpha_r):
    import numpy as np
    import concourse.bacc as bacc
    from concourse.bass_utils import run_bass_kernel_spmd

    NB, CI, HW, _ = x.shape
    C = L0_tok_conv_w.shape[0]
    NT = x_txt.shape[1]
    side = HW // PATCH
    grid = int(round(L0_tok_pos_table.shape[0] ** 0.5))
    kt = CI * PATCH * PATCH // P
    img = np.asarray(x).reshape(NB, CI, side, PATCH, side, PATCH).transpose(0, 1, 3, 5, 2, 4)
    img = img.reshape(NB, kt, P, side * side).transpose(0, 2, 1, 3)
    convw = np.asarray(L0_tok_conv_w).reshape(C, kt, P).transpose(2, 1, 0)
    edges = np.arange(1.0 / grid, 1.0, 1.0 / grid, dtype=np.float32)
    frac = np.arange(0.0, 1.0 - 1e-06, 1.0 / side, dtype=np.float32)
    bucket = np.searchsorted(edges, frac, side="right")
    pos_id = (bucket[:, None] * grid + bucket).reshape(2, -1).T.astype(np.int32)

    arrays = {
        "img": img, "txt": x_txt, "convw": convw, "convb": L0_tok_conv_b, "pos": L0_tok_pos_table, "pos_id": pos_id,
        "emb": L0_txt_emb, "w_in": L0_attn_W_in, "w_x": L0_attn_W_x, "w_dt": L0_attn_W_dt, "b_dt": np.asarray(L0_attn_b_dt).reshape(-1, P).T,
        "a_log": L0_attn_A_log, "d_skip": np.asarray(L0_attn_D_skip).reshape(-1, P).T, "w_out": L0_attn_W_out, "gamma": L0_attn_gamma,
        "beta": L0_attn_beta, "w_fc_t": np.asarray(L0_ffn_w_fc).T, "b_fc": np.asarray(L0_ffn_b_fc).reshape(-1, P).T,
        "w_proj_t": np.asarray(L0_ffn_w_proj).T, "b_proj": L0_ffn_b_proj, "alpha_e": L0_ffn_alpha_e,
        "alpha_r": L0_ffn_alpha_r,
    }
    arrays = {k + "_dram": np.ascontiguousarray(v) for k, v in arrays.items()}
    nc = bacc.Bacc("TRN2", target_bir_lowering=False, num_devices=1)
    args = [nc.dram_tensor(k, v.shape, mybir.dt.from_np(v.dtype), kind="ExternalInput").ap() for k, v in arrays.items()]
    out = nc.dram_tensor("out_dram", (NB, side * side + NT, C), F32, kind="ExternalOutput").ap()
    build(nc, *args, out)
    r = run_bass_kernel_spmd(nc, [arrays], core_ids=[0])
    return r.results[0]["out_dram"]
```
